# Optimizing a Trainium2 kernel written in Bass

```python
import numpy as np
import jax
import jax.numpy as jnp

def _softmax(x, axis=-1):
    return jax.nn.softmax(x, axis=axis)

def _gelu(x):
    return jax.nn.gelu(x, approximate=True)

def _silu(x):
    return jax.nn.silu(x)

def _sigmoid(x):
    return jax.nn.sigmoid(x)

def _layernorm(x, axis=-1, eps=1e-05):
    m = jnp.mean(x, axis=axis, keepdims=True)
    v = jnp.var(x, axis=axis, keepdims=True)
    return (x - m) / jnp.sqrt(v + eps)

def _scatter_add(tgt, idx, src, axis=0):
    return tgt.at[idx].add(src)

def _segment_sum(src, seg, n):
    return jax.ops.segment_sum(src, seg, n)
kernel_name = 'mk_prb_d1_jaxref_r2_07ff84'

def setup_inputs(seed: int=0):
    np.random.seed(seed)
    _w = jnp.asarray

    def _L0_attn_setup():
        import jax, jax.numpy as jnp
        import numpy as np
        N_HEAD = 16
        Q_DIM = 64
        V_DIM = 64
        WINDOW = 129
        DIL = 1
        key = jax.random.key(seed)
        ks = jax.random.split(key, 9)
        B, N, E = (1, 1024, 512)
        s = 0.02
        return {'x': jax.random.normal(ks[0], (B, N, E), jnp.float32), 'Wq': jax.random.normal(ks[1], (E, N_HEAD * Q_DIM), jnp.float32) * s, 'bq': jax.random.normal(ks[2], (N_HEAD * Q_DIM,), jnp.float32) * s, 'Wk': jax.random.normal(ks[3], (E, N_HEAD * Q_DIM), jnp.float32) * s, 'bk': jax.random.normal(ks[4], (N_HEAD * Q_DIM,), jnp.float32) * s, 'Wv': jax.random.normal(ks[5], (E, N_HEAD * V_DIM), jnp.float32) * s, 'bv': jax.random.normal(ks[6], (N_HEAD * V_DIM,), jnp.float32) * s, 'Wo': jax.random.normal(ks[7], (N_HEAD * V_DIM, E), jnp.float32) * s, 'bo': jax.random.normal(ks[8], (E,), jnp.float32) * s}
    _L0_attn_in = _L0_attn_setup()

    def _L0_ffn_setup():
        import jax, jax.numpy as jnp
        import numpy as np
        D_MODEL = 512
        M = 64
        INNER = 16
        key = jax.random.key(seed)
        ks = jax.random.split(key, 9)

        def init(k, shape, fan_in):
            bound = 1.0 / np.sqrt(fan_in)
            return jax.random.uniform(k, shape, jnp.float32, -bound, bound)
        x = jax.random.normal(ks[0], (16, 2048, D_MODEL), dtype=jnp.float32)
        Win = init(ks[1], (D_MODEL, M), D_MODEL)
        bin_ = init(ks[2], (M,), D_MODEL)
        W1 = init(ks[3], (M, INNER), 1)
        b1 = init(ks[4], (M, INNER), 1)
        W2 = init(ks[5], (M, INNER), INNER)
        b2 = init(ks[6], (M,), INNER)
        Wout = init(ks[7], (M, D_MODEL), M)
        bout = init(ks[8], (D_MODEL,), M)
        return {'x': x, 'Win': Win, 'bin_': bin_, 'W1': W1, 'b1': b1, 'W2': W2, 'b2': b2, 'Wout': Wout, 'bout': bout}
    _L0_ffn_in = _L0_ffn_setup()
    _d = {'L0_attn_x': _L0_attn_in['x'], 'L0_attn_Wq': _L0_attn_in['Wq'], 'L0_attn_bq': _L0_attn_in['bq'], 'L0_attn_Wk': _L0_attn_in['Wk'], 'L0_attn_bk': _L0_attn_in['bk'], 'L0_attn_Wv': _L0_attn_in['Wv'], 'L0_attn_bv': _L0_attn_in['bv'], 'L0_attn_Wo': _L0_attn_in['Wo'], 'L0_attn_bo': _L0_attn_in['bo'], 'L0_ffn_Win': _L0_ffn_in['Win'], 'L0_ffn_bin_': _L0_ffn_in['bin_'], 'L0_ffn_W1': _L0_ffn_in['W1'], 'L0_ffn_b1': _L0_ffn_in['b1'], 'L0_ffn_W2': _L0_ffn_in['W2'], 'L0_ffn_b2': _L0_ffn_in['b2'], 'L0_ffn_Wout': _L0_ffn_in['Wout'], 'L0_ffn_bout': _L0_ffn_in['bout']}
    _x0 = _d['L0_attn_x']
    _d['L0_attn_x'] = jax.random.normal(jax.random.fold_in(jax.random.key(seed), 1), (8, 1024, 512), dtype=_x0.dtype)
    del _x0
    return _d

def reference(L0_attn_x, L0_attn_Wq, L0_attn_bq, L0_attn_Wk, L0_attn_bk, L0_attn_Wv, L0_attn_bv, L0_attn_Wo, L0_attn_bo, L0_ffn_Win, L0_ffn_bin_, L0_ffn_W1, L0_ffn_b1, L0_ffn_W2, L0_ffn_b2, L0_ffn_Wout, L0_ffn_bout):

    def _L0_attn_ref(x, Wq, bq, Wk, bk, Wv, bv, Wo, bo):
        import jax, jax.numpy as jnp
        import numpy as np
        N_HEAD = 16
        Q_DIM = 64
        V_DIM = 64
        WINDOW = 129
        DIL = 1
        B, N, E = x.shape
        Q = (x @ Wq + bq).reshape(B, N, N_HEAD, Q_DIM).transpose(0, 2, 1, 3)
        K = (x @ Wk + bk).reshape(B, N, N_HEAD, Q_DIM).transpose(0, 2, 1, 3)
        V = (x @ Wv + bv).reshape(B, N, N_HEAD, V_DIM).transpose(0, 2, 1, 3)
        scores = jnp.einsum('bhid,bhjd->bhij', Q, K)
        idx = jnp.arange(N)
        diff = idx[None, :] - idx[:, None]
        half = WINDOW // 2
        band = (jnp.abs(diff) <= half * DIL) & (diff % DIL == 0)
        columns = jnp.where(band[None, None], scores, jnp.float32(0.0))
        attn = jax.nn.softmax(columns, axis=-1)
        out = attn @ V
        out = out.transpose(0, 2, 1, 3).reshape(B, N, N_HEAD * V_DIM)
        return out @ Wo + bo

    def _L0_ffn_ref(x, Win, bin_, W1, b1, W2, b2, Wout, bout):
        import jax, jax.numpy as jnp
        import numpy as np
        D_MODEL = 512
        M = 64
        INNER = 16
        s = jnp.einsum('btd,dm->btm', x, Win) + bin_
        h = jax.nn.relu(s[..., None] * W1 + b1)
        g = jnp.einsum('btmh,mh->btm', h, W2) + b2
        out = jnp.einsum('btm,md->btd', g, Wout) + bout
        return out
    x = L0_attn_x
    xn = _layernorm(x, axis=-1)
    x = x + _L0_attn_ref(xn, L0_attn_Wq, L0_attn_bq, L0_attn_Wk, L0_attn_bk, L0_attn_Wv, L0_attn_bv, L0_attn_Wo, L0_attn_bo) + _L0_ffn_ref(xn, L0_ffn_Win, L0_ffn_bin_, L0_ffn_W1, L0_ffn_b1, L0_ffn_W2, L0_ffn_b2, L0_ffn_Wout, L0_ffn_bout)
    return x

_drawn_inputs = setup_inputs


def setup_inputs(seed=0):
    import zlib

    import numpy as np

    out = dict(_drawn_inputs(seed))
    spreads = {}
    factors = {'L0_attn_bq': 25.596,
     'L0_attn_bk': 41.617,
     'L0_attn_bv': 4.228,
     'L0_attn_bo': 3.025,
     'L0_ffn_bin_': 8.0}
    for name, (base, spread) in spreads.items():
        noise = np.random.default_rng([zlib.crc32(name.encode()), seed]).standard_normal(out[name].shape)
        drawn = base * np.exp(spread * noise) if base else spread * noise
        out[name] = jnp.asarray(drawn.astype(out[name].dtype))
    for name, factor in factors.items():
        out[name] = (out[name] * factor).astype(out[name].dtype)
    return out
```

```python
from contextlib import ExitStack

import concourse.bass as bass
from concourse import mybir

F32 = mybir.dt.float32
F32R = mybir.dt.float32r
ALU = mybir.AluOpType
ACT = mybir.ActivationFunctionType

P = 128


def begun(count):
    return not isinstance(count, int) or count > 0


def in_register(engine, count):
    return count if isinstance(count, int) else engine.to_reg(count)


def band_attention_ffn(nc, x, Wq, bq, Wk, bk, Wv, bv, Wo, bo, Win, bin_, W1, b1, W2, b2, Wout, bout, out):
    B, N, E = x.shape
    HD = Wq.shape[1]
    D = 64
    PAIRS = HD // P
    M, INNER = W1.shape
    T = N // P
    KC = E // P
    HALF = 64
    WIN = 2 * P
    LINE = N // 2
    HQ = INNER // 2
    EPS = 1e-5
    assert (E, N, HD, M, B) == (4 * P, 8 * P, 1024, 64, 8) and HALF + P <= WIN

    with ExitStack() as ctx:
        def sb(name, shape, dt=F32):
            return ctx.enter_context(nc.sbuf_tensor(name, shape, dt))

        def bank(name):
            return ctx.enter_context(nc.psum_tensor(name, [P, 512], F32))

        def sem(name):
            return ctx.enter_context(nc.semaphore(name))

        acc = sb("acc", [P, 2, T, E])
        xn = sb("xn", [P, T, E])
        ffn = xn[:].rearrange("p t e -> p (t e)")
        ffn_s, ffn_g = ffn[:, 0:N], ffn[:, N:2 * N]
        ffn_h = [ffn[:, 2 * N:3 * N], ffn[:, 3 * N:4 * N]]
        xT = [sb(f"xT_{part}", [P, KC, N], F32R) for part in ("hi", "lo")]
        w_raw = sb("w_raw", [P, 3, KC, P])
        w = [sb(f"w_{part}", [P, 3, KC, P], F32R) for part in ("hi", "lo")]
        wo_raw = sb("wo_raw", [P, E])
        wo = [sb(f"wo_{part}", [P, E], F32R) for part in ("hi", "lo")]
        qT = [sb(f"qT_{part}", [P, N], F32R) for part in ("hi", "lo")]
        kT = [sb(f"kT_{part}", [P, N + 2 * HALF], F32R) for part in ("hi", "lo")]
        vT = sb("vT", [P, N])
        v = sb("v", [P, T, 2, 2, D], F32R)
        probs = sb("probs", [P, 2, T, WIN])
        pT = [[sb(f"pT{i}_{part}", [P, 2 * LINE], F32R) for part in ("hi", "lo")] for i in range(2)]
        o_part = [sb(f"o_part{i}", [P, LINE]) for i in range(2)]
        o_sum = [sb(f"o_sum{i}", [P, LINE]) for i in range(2)]
        oT = [sb(f"oT_{part}", [P, N], F32R) for part in ("hi", "lo")]
        mask = sb("mask", [P, WIN])
        ident = sb("ident", [P, P])
        bias_row = sb("bias_row", [P, E])
        bias_2 = sb("bias_2", [P, E])
        bias_rows = sb("bias_rows", [3 * PAIRS, P])
        bias_qkv = sb("bias_qkv", [P, 3, PAIRS, 1])
        win_raw = sb("win_raw", [P, KC, M])
        win = [sb(f"win_{part}", [P, KC, 2, M], F32R) for part in ("hi", "lo")]
        wout = sb("wout", [P, E])
        ffn_bin = sb("ffn_bin", [P, 1])
        w1c, b1c, w2c = sb("w1c", [P, HQ]), sb("b1c", [P, HQ]), sb("w2c", [P, HQ])
        b2c = sb("b2c", [P, 1])
        stats = sb("stats", [P, T, 6])
        mean_var = sb("mean_var", [P, T, 2])
        minus_half = sb("minus_half", [P, T])
        var_eps, rstd = sb("var_eps", [P, T]), sb("rstd", [P, T])
        mean_rstd, shift = sb("mean_rstd", [P, T]), sb("shift", [P, T])
        row_max, neg_max, row_sum, e0 = (sb(s, [P, 2 * T]) for s in ("row_max", "neg_max", "row_sum", "e0"))
        row_l, inv_l, neg_e = (sb(s, [P, 2 * T]) for s in ("row_l", "inv_l", "neg_e"))
        v_sums, v_mean, v_new = sb("v_sums", [P, 3]), sb("v_mean", [P, 2]), sb("v_new", [P, 1])
        v_back = sb("v_back", [P, 1])

        fill = [bank("fill0"), bank("fill1")]
        score = [bank("score0"), bank("score1")]
        pT_ps = [bank("pT_ps0"), bank("pT_ps1")]
        o_ps = [bank("o_ps0"), bank("o_ps1")]

        const_in = sem("const_in")
        bias_T, bias_in = sem("bias_T"), sem("bias_in")
        x_in, wo_in = sem("x_in"), sem("wo_in")
        w_in = [sem(f"w_in_{s}") for s in "vqk"]
        stored = sem("stored")
        pool_set, dve_set, win_ready = sem("pool_set"), sem("dve_set"), sem("win_ready")
        ln_stats, ln_agg, ln_small, xn_ready = sem("ln_stats"), sem("ln_agg"), sem("ln_small"), sem("xn_ready")
        xT_done, xT_hi, xT_lo = sem("xT_done"), sem("xT_hi"), sem("xT_lo")
        w_hi, w_lo = sem("w_hi"), sem("w_lo")
        wo_hi, wo_lo = sem("wo_hi"), sem("wo_lo")
        v_proj, v_in, v_stat, v_centered = sem("v_proj"), sem("v_in"), sem("v_stat"), sem("v_centered")
        v_back_ready = sem("v_back_ready")
        v_T, v_hi, v_lo = sem("v_T"), sem("v_hi"), sem("v_lo")
        qk_proj, qk_hi, qk_lo = sem("qk_proj"), sem("qk_hi"), sem("qk_lo")
        scored, masked, max_ready = sem("scored"), sem("masked"), sem("max_ready")
        exp_done, l_ready, inv_ready, norm_ready = sem("exp_done"), sem("l_ready"), sem("inv_ready"), sem("norm_ready")
        normed, p_T, pT_hi, pT_lo = sem("normed"), sem("p_T"), sem("pT_hi"), sem("pT_lo")
        pv_done, o_half, o_summed, oT_hi, oT_lo = (sem(s) for s in ("pv_done", "o_half", "o_summed", "oT_hi", "oT_lo"))
        out_done, out_added = sem("out_done"), sem("out_added")
        bias_added = sem("bias_added")
        ffn_in, ffn_s_in, ffn_relu, ffn_acc = sem("ffn_in"), sem("ffn_s_in"), sem("ffn_relu"), sem("ffn_acc")
        ffn_out, ffn_added = sem("ffn_out"), sem("ffn_added")

        hi, lo = 0, 1
        PASSES = [(hi, hi), (hi, lo), (lo, hi)]
        V_, Q_, K_ = 0, 1, 2
        OUT_BANK = (1, 0, 0, 1, 0, 1, 0, 0)
        QK_BANK = (0, 1, 1, 1)
        x_d = x.rearrange("b (t p) e -> b p t e", p=P)
        out_d = out.rearrange("b (t p) e -> b p t e", p=P)
        w_d = [m.rearrange("(k p) (h c) -> h p k c", p=P, c=P) for m in (Wv, Wq, Wk)]
        wo_d = Wo.rearrange("(h p) e -> h p e", p=P)
        N_CONST = 3 + 1 + 2 * 5 + 1 + 2

        def f32(a):
            return a.bitcast(F32)

        def column(tp, h, i):
            return 4 * tp + 2 * h + i

        def tiles_of(half):
            return range(4 * half, 4 * half + 4)

        def run_steps(engine, step):
            def middle(b):
                with engine.Fori(2, PAIRS - 1) as pair:
                    step(b * PAIRS + pair, b, pair)

            step(0, 0, 0, attend=False, out_proj=False, ln=True, ffn_first=True)
            step(1, 0, 1, out_proj=False, ffn_last=True)
            middle(0)
            with engine.Fori(1, B) as b:
                step(b * PAIRS - 1, b - 1, PAIRS - 1, ln_next=True)
                step(b * PAIRS, b, 0, ln=True, ffn_first=True)
                step(b * PAIRS + 1, b, 1, ffn_last=True)
                middle(b)
            step(B * PAIRS - 1, B - 1, PAIRS - 1, last=True)
            step(B * PAIRS, B, 0, proj=False, last=True)
            step(B * PAIRS + 1, B, 1, proj=False, attend=False, last=True)

        block = ctx.enter_context(nc.Block())

        @block.sync
        def _(sp):
            def load_weights(n, pair):
                for i in range(3):
                    if begun(3 * (n - 1) + i + 1):
                        sp.wait_ge(w_lo, 3 * (n - 1) + i + 1)
                    sp.dma_start(w_raw[:, i], w_d[i][pair]).then_inc(w_in[i], 16)

            def load_output_weights(n, pair):
                if begun(n):
                    sp.wait_ge(wo_lo, n)
                sp.dma_start(wo_raw[:], wo_d[pair]).then_inc(wo_in, 16)

            def store(b):
                sp.wait_ge(out_added, (b + 1) * PAIRS * T)
                sp.dma_start(out_d[b], acc[:, b % 2]).then_inc(stored, 16)

            sp.dma_start(acc[:, 0], x_d[0]).then_inc(x_in, 16)
            load_weights(0, 0)
            for i, m in enumerate((bv, bq, bk)):
                sp.dma_start(bias_rows[i * PAIRS:(i + 1) * PAIRS], m.rearrange("(h p) -> h p", p=P)).then_inc(const_in, 16)
            sp.dma_start(win_raw[:], Win.rearrange("(k p) m -> p k m", p=P)).then_inc(const_in, 16)
            for u in range(2):
                rows = slice(u * M, u * M + M)
                sp.dma_start(ffn_bin[rows], bin_.rearrange("(m o) -> m o", o=1)).then_inc(const_in, 16)
                for dst, src in ((w1c, W1), (b1c, b1), (w2c, W2)):
                    sp.dma_start(dst[rows], src[:, u * HQ:u * HQ + HQ]).then_inc(const_in, 16)
                sp.dma_start(wout[rows], Wout).then_inc(const_in, 16)
            sp.dma_start(b2c[0:M], b2.rearrange("(m o) -> m o", o=1)).then_inc(const_in, 16)
            sp.dma_start(bias_row[:], bo.rearrange("(o e) -> o e", o=1).broadcast_to([P, E])).then_inc(const_in, 16)
            sp.dma_start(bias_2[:], bout.rearrange("(o e) -> o e", o=1).broadcast_to([P, E])).then_inc(const_in, 16)
            sp.wait_ge(x_in, 16)
            sp.dma_start(acc[:, 1], x_d[1]).then_inc(x_in, 16)

            def step(n, b, pair, proj=True, ffn_last=False, last=False, **_):
                if not last:
                    load_weights(n + 1, (pair + 1) if not isinstance(pair, int) else (pair + 1) % PAIRS)
                if proj:
                    load_output_weights(n, pair)
                if ffn_last and not isinstance(b, int):
                    store(b - 1)
                    sp.wait_ge(stored, 16 * b)
                    sp.dma_start(acc[:, (b + 1) % 2], x_d[(b + 1) % B]).then_inc(x_in, 16)

            run_steps(sp, step)
            store(B - 1)
            sp.wait_ge(stored, 16 * B)
            sp.wait_ge(x_in, 16 * (B + 1))

        @block.gpsimd
        def _(pool):
            pool.memset(ident[:], 0.0).then_inc(pool_set, 1)
            pool.memset(mask[:], 1.0).then_inc(pool_set, 1)
            pool.memset(minus_half[:], -0.5).then_inc(pool_set, 1)
            pool.wait_ge(pool_set, 2)
            pool.affine_select(out=ident[:], in_=ident[:], compare_op=ALU.not_equal, fill=1.0, base=0,
                               pattern=[[-1, P]], channel_multiplier=1).then_inc(pool_set, 1)
            pool.affine_select(out=mask[:], in_=mask[:], compare_op=ALU.is_ge, fill=0.0, base=0,
                               pattern=[[1, WIN]], channel_multiplier=-1).then_inc(pool_set, 1)
            pool.wait_ge(pool_set, 5)
            pool.affine_select(out=mask[:], in_=mask[:], compare_op=ALU.is_ge, fill=0.0, base=2 * HALF,
                               pattern=[[-1, WIN]], channel_multiplier=1).then_inc(pool_set, 1)

            def layer_norm(b):
                due = in_register(pool, b + 1)
                pool.wait_ge(ln_agg, 1)
                pool.wait_ge(ln_agg, due)
                pool.tensor_scalar(var_eps[:], mean_var[:, :, 1], EPS, None, ALU.add).then_inc(ln_small, 1)
                pool.wait_ge(ln_small, 4 * b + 1)
                pool.tensor_tensor(rstd[:], var_eps[:], minus_half[:], ALU.pow).then_inc(ln_small, 1)
                pool.wait_ge(ln_small, 4 * b + 2)
                pool.tensor_tensor(mean_rstd[:], mean_var[:, :, 0], rstd[:], ALU.mult).then_inc(ln_small, 1)
                due = in_register(pool, 4 * b + 3)
                pool.wait_ge(ln_small, 1)
                pool.wait_ge(ln_small, due)
                pool.tensor_scalar(shift[:], mean_rstd[:], -1.0, 0.0, ALU.mult, ALU.add).then_inc(ln_small, 1)

            def split_low(n, i):
                pool.wait_ge(w_hi, 3 * n + i + 1)
                pool.tensor_tensor(w[lo][:, i], w_raw[:, i], f32(w[hi][:, i]), ALU.subtract).then_inc(w_lo, 1)

            for i in range(3):
                split_low(0, i)
            layer_norm(0)
            pool.wait_ge(const_in, 16 * N_CONST)
            pool.tensor_tensor(bias_row[:], bias_row[:], bias_2[:], ALU.add).then_inc(pool_set, 1)
            pool.wait_ge(pool_set, 7)

            def step(n, b, pair, attend=True, ln_next=False, ffn_first=False, ffn_last=False, last=False, **_):
                j = n - 1

                def normalise_weights(half):
                    due = in_register(pool, 2 * j + half + 1)
                    pool.wait_ge(norm_ready, 1)
                    pool.wait_ge(norm_ready, due)
                    for h in range(2):
                        for t in tiles_of(half):
                            c = column(t // 2, h, t % 2)
                            pool.tensor_scalar(probs[:, h, t], probs[:, h, t], inv_l[:, c:c + 1], neg_e[:, c:c + 1],
                                               ALU.mult, ALU.add).then_inc(normed, 1)

                def output_low(half):
                    cols = slice(half * LINE, half * LINE + LINE)
                    pool.wait_ge(oT_hi, 2 * j + half + 1)
                    pool.tensor_tensor(oT[lo][:, cols], o_sum[half][:], f32(oT[hi][:, cols]), ALU.subtract) \
                        .then_inc(oT_lo, 1)

                def add_biases(tiles):
                    pool.wait_ge(xn_ready, T * b + T)
                    for t in tiles:
                        pool.tensor_tensor(acc[:, b % 2, t], acc[:, b % 2, t], bias_row[:], ALU.add) \
                            .then_inc(bias_added, 1)

                if attend:
                    normalise_weights(0)
                if not last:
                    split_low(n + 1, V_)
                if ln_next:
                    layer_norm(b + 1)
                if attend:
                    normalise_weights(1)
                if ffn_last:
                    add_biases(tiles_of(1))
                if not last:
                    split_low(n + 1, Q_)
                if attend:
                    output_low(0)
                    pool.wait_ge(wo_hi, j + 1)
                    pool.tensor_tensor(wo[lo][:], wo_raw[:], f32(wo[hi][:]), ALU.subtract).then_inc(wo_lo, 1)
                    output_low(1)
                if not last:
                    split_low(n + 1, K_)
                if ffn_first:
                    add_biases(tiles_of(0))

            run_steps(pool, step)

        @block.scalar
        def _(act):
            def split_high(n, i, used, count):
                act.wait_ge(w_in[i], 16 * (n + 1))
                if begun(count):
                    act.wait_ge(used, count)
                act.activation(w[hi][:, i], w_raw[:, i], ACT.Copy).then_inc(w_hi, 1)

            def normalise(b, tiles):
                due = in_register(act, 4 * b + 4)
                act.wait_ge(ln_small, 1)
                act.wait_ge(ln_small, due)
                if begun(T * b):
                    due = in_register(act, T * b)
                    act.wait_ge(ffn_out, 1)
                    act.wait_ge(ffn_out, due)
                for t in tiles:
                    act.activation(xn[:, t], acc[:, b % 2, t], ACT.Identity, bias=shift[:, t:t + 1],
                                   scale=rstd[:, t:t + 1]).then_inc(xn_ready, 1)

            for i in range(3):
                split_high(0, i, v_proj, 0)
            normalise(0, range(T))
            act.wait_ge(const_in, 16 * N_CONST)
            act.wait_ge(bias_T, 1)
            act.activation(bias_qkv[:].rearrange("p i h o -> p (i h o)"), fill[0][:, 0:3 * PAIRS], ACT.Copy) \
                .then_inc(bias_in, 1)
            act.wait_ge(bias_in, 1)

            def step(n, b, pair, proj=True, attend=True, ln=False, ln_next=False, ffn_first=False, ffn_last=False,
                     last=False, **_):
                j, o = n - 1, n - 2

                def exps(tp):
                    act.wait_ge(max_ready, 4 * j + tp + 1)
                    for h in range(2):
                        for i in range(2):
                            c, t = column(tp, h, i), 2 * tp + i
                            act.activation(probs[:, h, t], probs[:, h, t], ACT.Exp, bias=neg_max[:, c:c + 1],
                                           accum_out=row_sum[:, c:c + 1])
                    cols = slice(4 * tp, 4 * tp + 4)
                    act.activation(e0[:, cols], neg_max[:, cols], ACT.Exp).then_inc(exp_done, 1)

                def relu(q):
                    if q == 0:
                        act.wait_ge(ffn_s_in, 2 * b + 2)
                    if begun(HQ * b + q - 1):
                        act.wait_ge(ffn_acc, HQ * b + q - 1)
                    act.activation(ffn_h[q % 2], ffn_s, ACT.Relu, bias=b1c[:, q:q + 1], scale=w1c[:, q:q + 1]) \
                        .then_inc(ffn_relu, 1)

                def value_lines(half):
                    act.wait_ge(v_proj, 2 * n + half + 1)
                    if half == 0:
                        act.activation(vT[:, HALF:HALF + LINE], fill[0][:], ACT.Identity,
                                       accum_out=v_sums[:, 0:1]).then_inc(v_in, 1)
                    else:
                        act.activation(vT[:, HALF + LINE:N], fill[1][:, 0:LINE - HALF], ACT.Identity,
                                       accum_out=v_sums[:, 1:2])
                        act.activation(vT[:, 0:HALF], fill[1][:, LINE - HALF:LINE], ACT.Identity,
                                       accum_out=v_sums[:, 2:3]).then_inc(v_in, 1)

                def qk_high(i):
                    dst, half = (qT[hi][:], i % 2) if i < 2 else (kT[hi][:, HALF:HALF + N], i % 2)
                    due = in_register(act, 4 * n + i + 1)
                    act.wait_ge(qk_proj, 1)
                    act.wait_ge(qk_proj, due)
                    act.activation(dst[:, half * LINE:half * LINE + LINE], fill[QK_BANK[i]][:], ACT.Identity,
                                   bias=bias_qkv[:, Q_ + i // 2, pair]).then_inc(qk_hi, 1)

                def weights_high(u):
                    if begun(4 * j + u - 1):
                        act.wait_ge(pv_done, 4 * j + u - 1)
                    for k in range(2):
                        act.wait_ge(p_T, 8 * j + 2 * u + k + 1)
                        act.activation(pT[u % 2][hi][:, k * LINE:k * LINE + LINE], pT_ps[k][:], ACT.Copy) \
                            .then_inc(pT_hi, 1)

                def output_half(u):
                    h = u % 2
                    act.wait_ge(pv_done, 4 * j + u + 1)
                    act.activation(o_part[h][h * D:h * D + D], o_ps[h][D - h * D:2 * D - h * D], ACT.Copy) \
                        .then_inc(o_half, 1)

                def output_high(half):
                    act.wait_ge(o_summed, 4 * j + 2 * half + 2)
                    if begun(T * o + 4 * half + 4):
                        act.wait_ge(out_done, T * o + 4 * half + 4)
                    act.activation(oT[hi][:, half * LINE:half * LINE + LINE], o_sum[half][:], ACT.Copy) \
                        .then_inc(oT_hi, 1)

                def x_high(items):
                    for i in items:
                        half, k = i // KC, i % KC
                        act.wait_ge(xT_done, T * b + i + 1)
                        act.activation(xT[hi][:, k, half * LINE:half * LINE + LINE], fill[i % 2][:], ACT.Copy) \
                            .then_inc(xT_hi, 1)

                if attend:
                    exps(0)
                if ffn_last:
                    relu(4)
                if ln:
                    x_high(range(0, KC))
                if proj:
                    value_lines(0)
                if ln:
                    x_high(range(KC, T))
                if attend:
                    exps(1)
                if ffn_last:
                    relu(5)
                if proj:
                    value_lines(1)
                if attend:
                    exps(2)
                if ffn_last:
                    relu(6)
                if not last:
                    split_high(n + 1, V_, v_proj, 2 * n + 2)
                if attend:
                    exps(3)
                for half in range(2) if ffn_first else ():
                    act.wait_ge(ffn_in, 2 * b + half + 1)
                    act.activation(ffn_s[:, half * LINE:half * LINE + LINE], fill[half][:], ACT.Identity,
                                   bias=ffn_bin[:]).then_inc(ffn_s_in, 1)
                if ffn_last:
                    relu(7)
                for u in range(4):
                    if attend:
                        weights_high(u)
                        if u:
                            output_half(u - 1)
                    if proj:
                        qk_high(u)
                    if u == 2 and not last:
                        split_high(n + 1, Q_, qk_proj, 4 * n + 2)
                    if u == 2 and attend:
                        output_high(0)
                    if ffn_first:
                        relu(u)
                    if ln_next:
                        normalise(b + 1, range(2 * u, 2 * u + 2))
                if attend:
                    act.wait_ge(wo_in, 16 * (j + 1))
                    if begun(T * j):
                        act.wait_ge(out_done, T * j)
                    act.activation(wo[hi][:], wo_raw[:], ACT.Copy).then_inc(wo_hi, 1)
                    output_half(3)
                for i in range(2) if proj else ():
                    act.wait_ge(v_T, 2 * n + i + 1)
                    act.activation(v[:, 4 * i:4 * i + 4, :, hi, :].rearrange("p c h d -> p (c h) d"),
                                   fill[i][:].rearrange("p (c d) -> p c d", d=D), ACT.Copy).then_inc(v_hi, 1)
                if attend:
                    output_high(1)
                if not last:
                    split_high(n + 1, K_, qk_proj, 4 * n + 4)

            run_steps(act, step)

        @block.vector
        def _(dve):
            for part in (hi, lo):
                dve.memset(f32(kT[part][:, 0:HALF]), 0.0).then_inc(dve_set, 1)
                dve.memset(f32(kT[part][:, HALF + N:]), 0.0).then_inc(dve_set, 1)
            dve.memset(b2c[M:2 * M], 0.0).then_inc(dve_set, 1)

            def statistics(b, tiles):
                due = in_register(dve, 16 * (b + 1))
                dve.wait_ge(x_in, 1)
                dve.wait_ge(x_in, due)
                for t in tiles:
                    dve.bn_stats(stats[:, t], acc[:, b % 2, t]).then_inc(ln_stats, 1)

            def mean_and_variance(b):
                due = in_register(dve, T * (b + 1))
                dve.wait_ge(ln_stats, 1)
                dve.wait_ge(ln_stats, due)
                for t in range(T):
                    last = dve.bn_aggr(mean_var[:, t], stats[:, t])
                last.then_inc(ln_agg, 1)

            statistics(0, range(T))
            mean_and_variance(0)
            dve.wait_ge(const_in, 16 * N_CONST)
            for u in range(2):
                dve.tensor_copy(win[hi][:, :, u], win_raw[:]).then_inc(dve_set, 1)
            dve.wait_ge(dve_set, 7)
            for u in range(2):
                dve.tensor_tensor(win[lo][:, :, u], win_raw[:], f32(win[hi][:, :, u]), ALU.subtract) \
                    .then_inc(win_ready, 1)

            def step(n, b, pair, proj=True, attend=True, out_proj=True, ln=False, ln_next=False, ffn_first=False,
                     ffn_last=False, **_):
                j, o = n - 1, n - 2
                parity = (b + 1) % 2 if isinstance(pair, int) and pair < 2 else b % 2

                def mask_scores(tp):
                    due = in_register(dve, 4 * j + tp + 1)
                    dve.wait_ge(scored, 1)
                    dve.wait_ge(scored, due)
                    for h in range(2):
                        for i in range(2):
                            c, t = column(tp, h, i), 2 * tp + i
                            dve.tensor_tensor_reduce(out=probs[:, h, t], in0=score[h][:, i * WIN:i * WIN + WIN],
                                                     in1=mask[:], scale=1.0, scalar=0.0, op0=ALU.mult, op1=ALU.max,
                                                     accum_out=row_max[:, c:c + 1]).then_inc(masked, 1)
                    dve.wait_ge(masked, 16 * j + 4 * tp + 4)
                    cols = slice(4 * tp, 4 * tp + 4)
                    dve.tensor_scalar(neg_max[:, cols], row_max[:, cols], -1.0, None, ALU.mult).then_inc(max_ready, 1)

                def denominators(half):
                    cols = slice(T * half, T * half + T)
                    dve.wait_ge(exp_done, 4 * j + 2 * half + 2)
                    dve.scalar_tensor_tensor(row_l[:, cols], e0[:, cols], float(N - WIN), row_sum[:, cols],
                                             ALU.mult, ALU.add).then_inc(l_ready, 1)
                    dve.wait_ge(l_ready, 2 * j + half + 1)
                    dve.reciprocal(inv_l[:, cols], row_l[:, cols]).then_inc(inv_ready, 1)
                    dve.wait_ge(inv_ready, 2 * j + half + 1)
                    dve.scalar_tensor_tensor(neg_e[:, cols], e0[:, cols], -1.0, inv_l[:, cols],
                                             ALU.mult, ALU.mult).then_inc(norm_ready, 1)

                def add_output(tiles):
                    for t in tiles:
                        dve.wait_ge(out_done, T * o + t + 1)
                        dve.tensor_tensor(acc[:, parity, t], fill[OUT_BANK[t]][:], acc[:, parity, t], ALU.add) \
                            .then_inc(out_added, 1)

                def hidden(q):
                    dve.wait_ge(ffn_relu, HQ * b + q + 1)
                    if q == 0:
                        dve.tensor_scalar(ffn_g, ffn_h[0], w2c[:, 0:1], b2c[:], ALU.mult, ALU.add).then_inc(ffn_acc, 1)
                    else:
                        dve.wait_ge(ffn_acc, HQ * b + q)
                        dve.scalar_tensor_tensor(ffn_g, ffn_h[q % 2], w2c[:, q:q + 1], ffn_g, ALU.mult, ALU.add) \
                            .then_inc(ffn_acc, 1)

                def qk_low(i):
                    part = [(qT[p][:] if i < 2 else kT[p][:, HALF:HALF + N])[:, i % 2 * LINE:i % 2 * LINE + LINE]
                            for p in (hi, lo)]
                    dve.wait_ge(qk_hi, 4 * n + i + 1)
                    dve.scalar_tensor_tensor(part[lo], fill[QK_BANK[i]][:], bias_qkv[:, Q_ + i // 2, pair],
                                             f32(part[hi]), ALU.add, ALU.subtract).then_inc(qk_lo, 1)

                def weights_low(u):
                    for k in range(2):
                        cols = slice(k * LINE, k * LINE + LINE)
                        dve.wait_ge(pT_hi, 8 * j + 2 * u + k + 1)
                        dve.tensor_tensor(pT[u % 2][lo][:, cols], pT_ps[k][:], f32(pT[u % 2][hi][:, cols]),
                                          ALU.subtract).then_inc(pT_lo, 1)

                def output_sum(u):
                    h, half = u % 2, u // 2
                    rows = slice(h * D, h * D + D)
                    dve.wait_ge(o_half, 4 * j + u + 1)
                    dve.wait_ge(v_back_ready, j + 1)
                    if h == 0 and begun(2 * j - 1 + half):
                        dve.wait_ge(oT_lo, 2 * j - 1 + half)
                    dve.scalar_tensor_tensor(o_sum[half][rows], o_ps[h][rows], v_back[rows], o_part[h][rows],
                                             ALU.add, ALU.add).then_inc(o_summed, 1)

                def x_low(items):
                    for i in items:
                        half, k = i // KC, i % KC
                        cols = slice(half * LINE, half * LINE + LINE)
                        dve.wait_ge(xT_hi, T * b + i + 1)
                        dve.tensor_tensor(xT[lo][:, k, cols], fill[i % 2][:], f32(xT[hi][:, k, cols]), ALU.subtract) \
                            .then_inc(xT_lo, 1)

                if attend:
                    mask_scores(0)
                if ln:
                    x_low(range(0, KC))
                if ln_next:
                    statistics(b + 1, tiles_of(0))
                if out_proj:
                    add_output([0])
                if ln:
                    x_low(range(KC, T))
                if attend:
                    mask_scores(1)
                if ln_next:
                    statistics(b + 1, tiles_of(1))
                if out_proj:
                    add_output([1])
                if ffn_last:
                    hidden(4)
                if attend:
                    denominators(0)
                    mask_scores(2)
                if out_proj:
                    add_output([2, 3])
                if ffn_last:
                    hidden(5)
                if ln_next:
                    mean_and_variance(b + 1)
                if attend:
                    mask_scores(3)
                if out_proj:
                    add_output([4, 5])
                if ffn_last:
                    hidden(6)
                if proj:
                    dve.wait_ge(v_in, 2 * n + 2)
                    dve.tensor_tensor(v_mean[:, 0:1], v_sums[:, 0:1], v_sums[:, 1:2], ALU.add).then_inc(v_stat, 1)
                    dve.wait_ge(v_stat, 3 * n + 1)
                    dve.tensor_tensor(v_mean[:, 1:2], v_mean[:, 0:1], v_sums[:, 2:3], ALU.add).then_inc(v_stat, 1)
                    dve.wait_ge(v_stat, 3 * n + 2)
                    dve.tensor_scalar(v_new[:], v_mean[:, 1:2], 1.0 / N, None, ALU.mult).then_inc(v_stat, 1)
                    dve.wait_ge(v_stat, 3 * n + 3)
                    dve.tensor_scalar(vT[:], vT[:], v_new[:], None, ALU.subtract).then_inc(v_centered, 1)
                if attend:
                    denominators(1)
                if ffn_last:
                    hidden(7)
                for u in range(4):
                    if attend:
                        weights_low(u)
                        if u:
                            output_sum(u - 1)
                    if out_proj and u >= 2:
                        add_output([u + 4])
                    if proj:
                        qk_low(u)
                    if ffn_first:
                        hidden(u)
                if attend:
                    output_sum(3)
                if proj:
                    if attend:
                        dve.wait_ge(o_summed, 4 * j + 4)
                    dve.tensor_tensor(v_back[:], v_new[:], bias_qkv[:, V_, pair], ALU.add).then_inc(v_back_ready, 1)
                for t in range(T) if ffn_last else ():
                    dve.wait_ge(ffn_out, T * b + t + 1)
                    dve.wait_ge(bias_added, T * b + t + 1)
                    dve.tensor_tensor(acc[:, b % 2, t], fill[t % 2][:], acc[:, b % 2, t], ALU.add) \
                        .then_inc(ffn_added, 1)
                for i in range(2) if proj else ():
                    part = [v[:, 4 * i:4 * i + 4, :, p, :].rearrange("p c h d -> p (c h) d") for p in (hi, lo)]
                    dve.wait_ge(v_hi, 2 * n + i + 1)
                    dve.tensor_tensor(part[lo], fill[i][:].rearrange("p (c d) -> p c d", d=D), f32(part[hi]),
                                      ALU.subtract).then_inc(v_lo, 1)

            run_steps(dve, step)

        @block.tensor
        def _(pe):
            pe.wait_ge(pool_set, 6)
            pe.wait_ge(dve_set, 5)
            pe.wait_ge(win_ready, 2)
            pe.wait_ge(const_in, 16 * N_CONST)
            pe.transpose(fill[0][:, 0:3 * PAIRS], bias_rows[:], ident[0:3 * PAIRS, 0:3 * PAIRS]).then_inc(bias_T, 1)
            pe.wait_ge(bias_in, 1)

            def step(n, b, pair, proj=True, attend=True, out_proj=True, ln=False, ffn_first=False, ffn_last=False,
                     **_):
                j, o = n - 1, n - 2
                def scores(tp):
                    if tp == 0:
                        pe.wait_ge(qk_lo, 4 * j + 4)
                    if begun(16 * j + 4 * tp):
                        pe.wait_ge(masked, 16 * j + 4 * tp)
                    for i in range(2):
                        t = 2 * tp + i
                        for a, (qp, kp) in enumerate(PASSES):
                            for h in range(2):
                                rows = slice(h * D, h * D + D)
                                last = pe.matmul(score[h][:, i * WIN:i * WIN + WIN], qT[qp][rows, t * P:t * P + P],
                                                 kT[kp][rows, t * P:t * P + WIN], start=(a == 0), stop=(a == 2))
                    last.then_inc(scored, 1)

                def project(i, half, done, dst):
                    pe.wait_ge(w_lo, 3 * n + i + 1)
                    for k in range(KC):
                        for a, (wp, xp) in enumerate(PASSES):
                            last = pe.matmul(dst[:], w[wp][:, i, k], xT[xp][:, k, half * LINE:half * LINE + LINE],
                                             start=(k == 0 and a == 0), stop=(k == KC - 1 and a == 2))
                    last.then_inc(done, 1)

                def project_out(t):
                    if t == 0:
                        pe.wait_ge(wo_lo, o + 1)
                    if t % 4 == 0:
                        pe.wait_ge(oT_lo, 2 * o + t // 4 + 1)
                    dst = fill[OUT_BANK[t]]
                    for a, (op, wp) in enumerate(PASSES):
                        last = pe.matmul(dst[:], oT[op][:, t * P:t * P + P], wo[wp][:], start=(a == 0), stop=(a == 2))
                    last.then_inc(out_done, 1)

                def transpose_x(i):
                    half, k = i // KC, i % KC
                    pe.wait_ge(xn_ready, T * b + 4 * half + 4)
                    for t in tiles_of(half):
                        last = pe.transpose(fill[i % 2][:, t % 4 * P:t % 4 * P + P], xn[:, t, k * P:k * P + P], ident[:])
                    last.then_inc(xT_done, 1)

                def network_in(half):
                    for k in range(KC):
                        for a, (wp, xp) in enumerate(PASSES):
                            last = pe.matmul(fill[half][:], win[wp][:, k].rearrange("p u m -> p (u m)"),
                                             xT[xp][:, k, half * LINE:half * LINE + LINE],
                                             start=(k == 0 and a == 0), stop=(k == KC - 1 and a == 2))
                    last.then_inc(ffn_in, 1)

                def transpose_values(i):
                    for c in range(4):
                        last = pe.transpose(fill[i][:, c * P:c * P + P], vT[:, (4 * i + c) * P:(4 * i + c + 1) * P],
                                            ident[:])
                    last.then_inc(v_T, 1)

                def transpose_weights(u):
                    half, h = u // 2, u % 2
                    pe.wait_ge(normed, 16 * j + 4 * u + 4)
                    for i in range(8):
                        t, c, k = 4 * half + i // 2, i % 2, i // 4
                        if i % 4 == 0 and begun(8 * j + 2 * u + k - 1):
                            pe.wait_ge(pT_lo, 8 * j + 2 * u + k - 1)
                        last = pe.transpose(pT_ps[k][:, i % 4 * P:i % 4 * P + P], probs[:, h, t, c * P:c * P + P],
                                            ident[:])
                        if i % 4 == 3:
                            last.then_inc(p_T, 1)

                def weigh_values(u):
                    half, h = u // 2, u % 2
                    pe.wait_ge(pT_lo, 8 * j + 2 * u + 2)
                    if u == 0:
                        pe.wait_ge(v_lo, 2 * j + 2)
                    if begun(4 * j + u - 1):
                        pe.wait_ge(o_summed, 4 * j + u - 1)
                    for k in range(5):
                        first, end = max(2 * k - 1, 0), min(2 * k + 1, 8)
                        q0 = max(k - 1, 0) * P
                        for part in (hi, lo):
                            last = pe.matmul(o_ps[h][:, q0:q0 + (end - first) * P],
                                             v[:, (4 * half + k) % T, h].rearrange("p a d -> p (a d)"),
                                             pT[h][part][:, first * P:end * P], start=(k == 0 and part == hi),
                                             stop=(k == 4 and part == lo), skip_group_check=True)
                    last.then_inc(pv_done, 1)

                if attend:
                    scores(0)
                if ln:
                    if begun(2 * n):
                        pe.wait_ge(v_lo, 2 * n)
                    transpose_x(0)
                    transpose_x(1)
                    for i in range(2, KC):
                        pe.wait_ge(xT_lo, T * b + i - 1)
                        transpose_x(i)
                if proj:
                    if ln:
                        pe.wait_ge(xT_lo, T * b + KC)
                    else:
                        pe.wait_ge(v_lo, 2 * n - 1)
                    project(V_, 0, v_proj, fill[0])
                if out_proj:
                    if not attend:
                        pe.wait_ge(out_added, T * o)
                    elif not ln:
                        pe.wait_ge(v_lo, 2 * n)
                    project_out(0)
                if ln:
                    pe.wait_ge(v_in, 2 * n + 1)
                    transpose_x(KC)
                    if out_proj:
                        pe.wait_ge(out_added, T * o + 1)
                    transpose_x(KC + 1)
                    for i in range(KC + 2, T):
                        pe.wait_ge(xT_lo, T * b + i - 1)
                        transpose_x(i)
                if attend:
                    scores(1)
                if ln:
                    pe.wait_ge(xT_lo, T * b + T)
                if out_proj:
                    if proj and not ln:
                        pe.wait_ge(v_in, 2 * n + 1)
                    elif attend and not proj:
                        pe.wait_ge(v_lo, 2 * n - 1)
                    project_out(1)
                if proj:
                    if out_proj and not ln:
                        pe.wait_ge(out_added, T * o + 1)
                    elif not ln:
                        pe.wait_ge(v_lo, 2 * n)
                    project(V_, 1, v_proj, fill[1])
                if attend:
                    scores(2)
                if out_proj:
                    pe.wait_ge(out_added, T * o + 2)
                    project_out(2)
                    if proj:
                        pe.wait_ge(v_in, 2 * n + 2)
                    project_out(3)
                if attend:
                    scores(3)
                if out_proj:
                    pe.wait_ge(out_added, T * o + 3)
                    project_out(4)
                    pe.wait_ge(out_added, T * o + 4)
                    project_out(5)
                if ffn_first:
                    if out_proj:
                        pe.wait_ge(out_added, T * o + 5)
                    network_in(0)
                    if out_proj:
                        pe.wait_ge(out_added, T * o + 6)
                    else:
                        pe.wait_ge(v_in, 2 * n + 2)
                    network_in(1)
                if attend:
                    transpose_weights(0)
                if proj:
                    if ffn_first:
                        pe.wait_ge(ffn_s_in, 2 * b + 1)
                    elif out_proj:
                        pe.wait_ge(out_added, T * o + 5)
                    else:
                        pe.wait_ge(v_in, 2 * n + 1)
                    project(Q_, 0, qk_proj, fill[QK_BANK[0]])
                if attend:
                    transpose_weights(1)
                    weigh_values(0)
                if proj:
                    if ffn_first:
                        pe.wait_ge(ffn_s_in, 2 * b + 2)
                    elif out_proj:
                        pe.wait_ge(out_added, T * o + 6)
                    else:
                        pe.wait_ge(v_in, 2 * n + 2)
                    project(Q_, 1, qk_proj, fill[QK_BANK[1]])
                if attend:
                    transpose_weights(2)
                    weigh_values(1)
                if out_proj:
                    if proj:
                        pe.wait_ge(qk_lo, 4 * n + 1)
                    else:
                        pe.wait_ge(out_added, T * o + 5)
                    project_out(6)
                if proj:
                    pe.wait_ge(qk_lo, 4 * n + 2)
                    project(K_, 0, qk_proj, fill[QK_BANK[2]])
                if attend:
                    transpose_weights(3)
                    weigh_values(2)
                if out_proj:
                    pe.wait_ge(out_added, T * o + 7)
                    project_out(7)
                if proj:
                    pe.wait_ge(qk_lo, 4 * n + 3)
                    project(K_, 1, qk_proj, fill[QK_BANK[3]])
                if attend:
                    weigh_values(3)
                if ffn_last:
                    pe.wait_ge(ffn_acc, HQ * b + HQ)
                for t in range(T) if ffn_last else ():
                    if t == 0 and out_proj:
                        pe.wait_ge(out_added, T * o + T)
                    elif t == 1:
                        pe.wait_ge(qk_lo, 4 * n + 4)
                    elif t > 1:
                        pe.wait_ge(ffn_added, T * b + t - 1)
                    pe.matmul(fill[t % 2][:], ffn_g[:, t * P:t * P + P], wout[:], start=True, stop=True).then_inc(ffn_out, 1)
                if proj:
                    pe.wait_ge(v_centered, n + 1)
                    if ffn_last:
                        pe.wait_ge(ffn_added, T * b + T - 1)
                    elif out_proj:
                        pe.wait_ge(out_added, T * o + T)
                    transpose_values(0)
                    if ffn_last:
                        pe.wait_ge(ffn_added, T * b + T)
                    else:
                        pe.wait_ge(qk_lo, 4 * n + 4)
                    transpose_values(1)

            run_steps(pe, step)


_INS = ["L0_attn_x", "L0_attn_Wq", "L0_attn_bq", "L0_attn_Wk", "L0_attn_bk", "L0_attn_Wv", "L0_attn_bv", "L0_attn_Wo",
        "L0_attn_bo", "L0_ffn_Win", "L0_ffn_bin_", "L0_ffn_W1", "L0_ffn_b1", "L0_ffn_W2", "L0_ffn_b2", "L0_ffn_Wout",
        "L0_ffn_bout"]


def kernel(**inputs):
    import numpy as np
    import concourse.bacc as bacc
    from concourse.bass_utils import run_bass_kernel_spmd

    nc = bacc.Bacc("TRN2", target_bir_lowering=False, num_devices=1)
    arrays, args = {}, []
    for name in _INS:
        a = np.ascontiguousarray(inputs[name])
        arrays[f"in_{name}"] = a
        args.append(nc.dram_tensor(f"in_{name}", a.shape, mybir.dt.from_np(a.dtype), kind="ExternalInput").ap())
    shape = inputs["L0_attn_x"].shape
    args.append(nc.dram_tensor("out_x", shape, F32, kind="ExternalOutput").ap())
    band_attention_ffn(nc, *args)
    return run_bass_kernel_spmd(nc, [arrays], core_ids=[0]).results[0]["out_x"]
```

```python
from contextlib import ExitStack

import concourse.bass as bass
from concourse import mybir

F32 = mybir.dt.float32
F32R = mybir.dt.float32r
ALU = mybir.AluOpType
ACT = mybir.ActivationFunctionType

P = 128


def begun(count):
    return not isinstance(count, int) or count > 0


def in_register(engine, count):
    return count if isinstance(count, int) else engine.to_reg(count)


def band_attention_ffn(nc, x, Wq, bq, Wk, bk, Wv, bv, Wo, bo, Win, bin_, W1, b1, W2, b2, Wout, bout, out):
    B, N, E = x.shape
    HD = Wq.shape[1]
    D = 64
    PAIRS = HD // P
    M, INNER = W1.shape
    T = N // P
    KC = E // P
    HALF = 64
    WIN = 2 * P
    LINE = N // 2
    HQ = INNER // 2
    EPS = 1e-5
    assert (E, N, HD, M, B) == (4 * P, 8 * P, 1024, 64, 8) and HALF + P <= WIN

    with ExitStack() as ctx:
        def sb(name, shape, dt=F32):
            return ctx.enter_context(nc.sbuf_tensor(name, shape, dt))

        def bank(name):
            return ctx.enter_context(nc.psum_tensor(name, [P, 512], F32))

        def sem(name):
            return ctx.enter_context(nc.semaphore(name))

        acc = sb("acc", [P, 2, T, E])
        xn = sb("xn", [P, T, E])
        ffn = xn[:].rearrange("p t e -> p (t e)")
        ffn_s, ffn_g = ffn[:, 0:N], ffn[:, N:2 * N]
        ffn_h = [ffn[:, 2 * N:3 * N], ffn[:, 3 * N:4 * N]]
        xT = [sb(f"xT_{part}", [P, KC, N], F32R) for part in ("hi", "lo")]
        w_raw = sb("w_raw", [P, 3, KC, P])
        w = [sb(f"w_{part}", [P, 3, KC, P], F32R) for part in ("hi", "lo")]
        wo_raw = sb("wo_raw", [P, E])
        wo = [sb(f"wo_{part}", [P, E], F32R) for part in ("hi", "lo")]
        qT = [sb(f"qT_{part}", [P, N], F32R) for part in ("hi", "lo")]
        kT = [sb(f"kT_{part}", [P, N + 2 * HALF], F32R) for part in ("hi", "lo")]
        vT = sb("vT", [P, N])
        v = sb("v", [P, T, 2, 2, D], F32R)
        probs = sb("probs", [P, 2, T, WIN])
        pT = [[sb(f"pT{i}_{part}", [P, 2 * LINE], F32R) for part in ("hi", "lo")] for i in range(2)]
        o_part = [sb(f"o_part{i}", [P, LINE]) for i in range(2)]
        o_sum = [sb(f"o_sum{i}", [P, LINE]) for i in range(2)]
        oT = [sb(f"oT_{part}", [P, N], F32R) for part in ("hi", "lo")]
        mask = sb("mask", [P, WIN])
        ident = sb("ident", [P, P])
        bias_row = sb("bias_row", [P, E])
        bias_2 = sb("bias_2", [P, E])
        bias_rows = sb("bias_rows", [3 * PAIRS, P])
        bias_qkv = sb("bias_qkv", [P, 3, PAIRS, 1])
        win_raw = sb("win_raw", [P, KC, M])
        win = [sb(f"win_{part}", [P, KC, 2, M], F32R) for part in ("hi", "lo")]
        wout = sb("wout", [P, E])
        ffn_bin = sb("ffn_bin", [P, 1])
        w1c, b1c, w2c = sb("w1c", [P, HQ]), sb("b1c", [P, HQ]), sb("w2c", [P, HQ])
        b2c = sb("b2c", [P, 1])
        stats = sb("stats", [P, T, 6])
        mean_var = sb("mean_var", [P, T, 2])
        minus_half = sb("minus_half", [P, T])
        var_eps, rstd = sb("var_eps", [P, T]), sb("rstd", [P, T])
        mean_rstd, shift = sb("mean_rstd", [P, T]), sb("shift", [P, T])
        row_max, neg_max, row_sum, e0 = (sb(s, [P, 2 * T]) for s in ("row_max", "neg_max", "row_sum", "e0"))
        row_l, inv_l, neg_e = (sb(s, [P, 2 * T]) for s in ("row_l", "inv_l", "neg_e"))
        v_sums, v_mean, v_new = sb("v_sums", [P, 3]), sb("v_mean", [P, 2]), sb("v_new", [P, 1])
        v_back = sb("v_back", [P, 1])

        fill = [bank("fill0"), bank("fill1")]
        score = [bank("score0"), bank("score1")]
        pT_ps = [bank("pT_ps0"), bank("pT_ps1")]
        o_ps = [bank("o_ps0"), bank("o_ps1")]

        x_banks = pT_ps + fill

        const_in = sem("const_in")
        bias_T, bias_in = sem("bias_T"), sem("bias_in")
        x_in, wo_in = sem("x_in"), sem("wo_in")
        w_in = [sem(f"w_in_{s}") for s in "vqk"]
        stored = sem("stored")
        pool_set, dve_set, win_ready = sem("pool_set"), sem("dve_set"), sem("win_ready")
        ln_stats, ln_agg, ln_small, xn_ready = sem("ln_stats"), sem("ln_agg"), sem("ln_small"), sem("xn_ready")
        xT_done, xT_hi, xT_lo = sem("xT_done"), sem("xT_hi"), sem("xT_lo")
        w_hi, w_lo = sem("w_hi"), sem("w_lo")
        wo_hi, wo_lo = sem("wo_hi"), sem("wo_lo")
        v_proj, v_in, v_stat, v_centered = sem("v_proj"), sem("v_in"), sem("v_stat"), sem("v_centered")
        v_back_ready = sem("v_back_ready")
        v_T, v_hi, v_lo = sem("v_T"), sem("v_hi"), sem("v_lo")
        qk_proj, qk_hi, qk_lo = sem("qk_proj"), sem("qk_hi"), sem("qk_lo")
        scored, masked, max_ready = sem("scored"), sem("masked"), sem("max_ready")
        exp_done, l_ready, inv_ready, norm_ready = sem("exp_done"), sem("l_ready"), sem("inv_ready"), sem("norm_ready")
        normed, p_T, pT_hi, pT_lo = sem("normed"), sem("p_T"), sem("pT_hi"), sem("pT_lo")
        pv_done, o_half, o_summed, oT_hi, oT_lo = (sem(s) for s in ("pv_done", "o_half", "o_summed", "oT_hi", "oT_lo"))
        out_done, out_added = sem("out_done"), sem("out_added")
        bias_added = sem("bias_added")
        ffn_in, ffn_s_in, ffn_relu, ffn_acc = sem("ffn_in"), sem("ffn_s_in"), sem("ffn_relu"), sem("ffn_acc")
        ffn_out, ffn_added = sem("ffn_out"), sem("ffn_added")

        hi, lo = 0, 1
        PASSES = [(hi, hi), (hi, lo), (lo, hi)]
        V_, Q_, K_ = 0, 1, 2
        OUT_BANK = (1, 0, 0, 0, 1, 0, 0, 0)
        QK_BANK = (1, 0, 1, 1)
        x_d = x.rearrange("b (t p) e -> b p t e", p=P)
        out_d = out.rearrange("b (t p) e -> b p t e", p=P)
        w_d = [m.rearrange("(k p) (h c) -> h p k c", p=P, c=P) for m in (Wv, Wq, Wk)]
        wo_d = Wo.rearrange("(h p) e -> h p e", p=P)
        N_CONST = 3 + 1 + 2 * 5 + 1 + 2

        def f32(a):
            return a.bitcast(F32)

        def column(tp, h, i):
            return 4 * tp + 2 * h + i

        def tiles_of(half):
            return range(4 * half, 4 * half + 4)

        def run_steps(engine, step):
            def middle(b):
                with engine.Fori(2, PAIRS - 1) as pair:
                    step(b * PAIRS + pair, b, pair)

            step(0, 0, 0, attend=False, out_proj=False, ln=True, ffn_first=True)
            step(1, 0, 1, out_proj=False, ffn_last=True)
            middle(0)
            with engine.Fori(1, B) as b:
                step(b * PAIRS - 1, b - 1, PAIRS - 1, ln_next=True)
                step(b * PAIRS, b, 0, ln=True, ffn_first=True)
                step(b * PAIRS + 1, b, 1, ffn_last=True)
                middle(b)
            step(B * PAIRS - 1, B - 1, PAIRS - 1, last=True)
            step(B * PAIRS, B, 0, proj=False, last=True)
            step(B * PAIRS + 1, B, 1, proj=False, attend=False, last=True)

        block = ctx.enter_context(nc.Block())

        @block.sync
        def _(sp):
            def load_weights(n, pair):
                for i in range(3):
                    if begun(3 * (n - 1) + i + 1):
                        sp.wait_ge(w_lo, 3 * (n - 1) + i + 1)
                    sp.dma_start(w_raw[:, i], w_d[i][pair]).then_inc(w_in[i], 16)

            def load_output_weights(n, pair):
                if begun(n):
                    sp.wait_ge(wo_lo, n)
                sp.dma_start(wo_raw[:], wo_d[pair]).then_inc(wo_in, 16)

            def store(b):
                sp.wait_ge(out_added, (b + 1) * PAIRS * T)
                sp.dma_start(out_d[b], acc[:, b % 2]).then_inc(stored, 16)

            sp.dma_start(acc[:, 0], x_d[0]).then_inc(x_in, 16)
            load_weights(0, 0)
            for i, m in enumerate((bv, bq, bk)):
                sp.dma_start(bias_rows[i * PAIRS:(i + 1) * PAIRS], m.rearrange("(h p) -> h p", p=P)).then_inc(const_in, 16)
            sp.dma_start(win_raw[:], Win.rearrange("(k p) m -> p k m", p=P)).then_inc(const_in, 16)
            for u in range(2):
                rows = slice(u * M, u * M + M)
                sp.dma_start(ffn_bin[rows], bin_.rearrange("(m o) -> m o", o=1)).then_inc(const_in, 16)
                for dst, src in ((w1c, W1), (b1c, b1), (w2c, W2)):
                    sp.dma_start(dst[rows], src[:, u * HQ:u * HQ + HQ]).then_inc(const_in, 16)
                sp.dma_start(wout[rows], Wout).then_inc(const_in, 16)
            sp.dma_start(b2c[0:M], b2.rearrange("(m o) -> m o", o=1)).then_inc(const_in, 16)
            sp.dma_start(bias_row[:], bo.rearrange("(o e) -> o e", o=1).broadcast_to([P, E])).then_inc(const_in, 16)
            sp.dma_start(bias_2[:], bout.rearrange("(o e) -> o e", o=1).broadcast_to([P, E])).then_inc(const_in, 16)
            sp.wait_ge(x_in, 16)
            sp.dma_start(acc[:, 1], x_d[1]).then_inc(x_in, 16)

            def step(n, b, pair, proj=True, ffn_last=False, last=False, **_):
                if not last:
                    load_weights(n + 1, (pair + 1) if not isinstance(pair, int) else (pair + 1) % PAIRS)
                if proj:
                    load_output_weights(n, pair)
                if ffn_last and not isinstance(b, int):
                    store(b - 1)
                    sp.wait_ge(stored, 16 * b)
                    sp.dma_start(acc[:, (b + 1) % 2], x_d[(b + 1) % B]).then_inc(x_in, 16)

            run_steps(sp, step)
            store(B - 1)
            sp.wait_ge(stored, 16 * B)
            sp.wait_ge(x_in, 16 * (B + 1))

        @block.gpsimd
        def _(pool):
            pool.memset(ident[:], 0.0).then_inc(pool_set, 1)
            pool.memset(mask[:], 1.0).then_inc(pool_set, 1)
            pool.memset(minus_half[:], -0.5).then_inc(pool_set, 1)
            pool.wait_ge(pool_set, 2)
            pool.affine_select(out=ident[:], in_=ident[:], compare_op=ALU.not_equal, fill=1.0, base=0,
                               pattern=[[-1, P]], channel_multiplier=1).then_inc(pool_set, 1)
            pool.affine_select(out=mask[:], in_=mask[:], compare_op=ALU.is_ge, fill=0.0, base=0,
                               pattern=[[1, WIN]], channel_multiplier=-1).then_inc(pool_set, 1)
            pool.wait_ge(pool_set, 5)
            pool.affine_select(out=mask[:], in_=mask[:], compare_op=ALU.is_ge, fill=0.0, base=2 * HALF,
                               pattern=[[-1, WIN]], channel_multiplier=1).then_inc(pool_set, 1)

            def layer_norm(b):
                due = in_register(pool, b + 1)
                pool.wait_ge(ln_agg, 1)
                pool.wait_ge(ln_agg, due)
                pool.tensor_scalar(var_eps[:], mean_var[:, :, 1], EPS, None, ALU.add).then_inc(ln_small, 1)
                pool.wait_ge(ln_small, 4 * b + 1)
                pool.tensor_tensor(rstd[:], var_eps[:], minus_half[:], ALU.pow).then_inc(ln_small, 1)
                pool.wait_ge(ln_small, 4 * b + 2)
                pool.tensor_tensor(mean_rstd[:], mean_var[:, :, 0], rstd[:], ALU.mult).then_inc(ln_small, 1)
                due = in_register(pool, 4 * b + 3)
                pool.wait_ge(ln_small, 1)
                pool.wait_ge(ln_small, due)
                pool.tensor_scalar(shift[:], mean_rstd[:], -1.0, 0.0, ALU.mult, ALU.add).then_inc(ln_small, 1)

            def split_low(n, i):
                pool.wait_ge(w_hi, 3 * n + i + 1)
                pool.tensor_tensor(w[lo][:, i], w_raw[:, i], f32(w[hi][:, i]), ALU.subtract).then_inc(w_lo, 1)

            for i in range(3):
                split_low(0, i)
            layer_norm(0)
            pool.wait_ge(const_in, 16 * N_CONST)
            pool.tensor_tensor(bias_row[:], bias_row[:], bias_2[:], ALU.add).then_inc(pool_set, 1)
            pool.wait_ge(pool_set, 7)

            def step(n, b, pair, attend=True, ln_next=False, ffn_first=False, ffn_last=False, last=False, **_):
                j = n - 1

                def normalise_weights(half):
                    due = in_register(pool, 2 * j + half + 1)
                    pool.wait_ge(norm_ready, 1)
                    pool.wait_ge(norm_ready, due)
                    for h in range(2):
                        for t in tiles_of(half):
                            c = column(t // 2, h, t % 2)
                            pool.tensor_scalar(probs[:, h, t], probs[:, h, t], inv_l[:, c:c + 1], neg_e[:, c:c + 1],
                                               ALU.mult, ALU.add).then_inc(normed, 1)

                def output_low(half):
                    cols = slice(half * LINE, half * LINE + LINE)
                    pool.wait_ge(oT_hi, 2 * j + half + 1)
                    pool.tensor_tensor(oT[lo][:, cols], o_sum[half][:], f32(oT[hi][:, cols]), ALU.subtract) \
                        .then_inc(oT_lo, 1)

                def add_biases(tiles):
                    pool.wait_ge(xn_ready, T * b + T)
                    for t in tiles:
                        pool.tensor_tensor(acc[:, b % 2, t], acc[:, b % 2, t], bias_row[:], ALU.add) \
                            .then_inc(bias_added, 1)

                if attend:
                    normalise_weights(0)
                if not last:
                    split_low(n + 1, V_)
                if ln_next:
                    layer_norm(b + 1)
                if attend:
                    normalise_weights(1)
                if ffn_first or ffn_last:
                    add_biases([0, 1] if ffn_first else [4, 5])
                if not last:
                    split_low(n + 1, Q_)
                if attend:
                    output_low(0)
                if ffn_first or ffn_last:
                    add_biases([2, 3] if ffn_first else [6, 7])
                if attend:
                    pool.wait_ge(wo_hi, j + 1)
                    pool.tensor_tensor(wo[lo][:], wo_raw[:], f32(wo[hi][:]), ALU.subtract).then_inc(wo_lo, 1)
                    output_low(1)
                if not last:
                    split_low(n + 1, K_)

            run_steps(pool, step)

        @block.scalar
        def _(act):
            def split_high(n, i, used, count):
                act.wait_ge(w_in[i], 16 * (n + 1))
                if begun(count):
                    act.wait_ge(used, count)
                act.activation(w[hi][:, i], w_raw[:, i], ACT.Copy).then_inc(w_hi, 1)

            def normalise(b, tiles):
                due = in_register(act, 4 * b + 4)
                act.wait_ge(ln_small, 1)
                act.wait_ge(ln_small, due)
                if begun(T * b):
                    due = in_register(act, T * b)
                    act.wait_ge(ffn_out, 1)
                    act.wait_ge(ffn_out, due)
                for t in tiles:
                    act.activation(xn[:, t], acc[:, b % 2, t], ACT.Identity, bias=shift[:, t:t + 1],
                                   scale=rstd[:, t:t + 1]).then_inc(xn_ready, 1)

            for i in range(3):
                split_high(0, i, v_proj, 0)
            normalise(0, range(T))
            act.wait_ge(const_in, 16 * N_CONST)
            act.wait_ge(bias_T, 1)
            act.activation(bias_qkv[:].rearrange("p i h o -> p (i h o)"), fill[0][:, 0:3 * PAIRS], ACT.Copy) \
                .then_inc(bias_in, 1)
            act.wait_ge(bias_in, 1)

            def step(n, b, pair, proj=True, attend=True, ln=False, ln_next=False, ffn_first=False, ffn_last=False,
                     last=False, **_):
                j, o = n - 1, n - 2

                def exps(tp):
                    act.wait_ge(max_ready, 4 * j + tp + 1)
                    for h in range(2):
                        for i in range(2):
                            c, t = column(tp, h, i), 2 * tp + i
                            act.activation(probs[:, h, t], probs[:, h, t], ACT.Exp, bias=neg_max[:, c:c + 1],
                                           accum_out=row_sum[:, c:c + 1])
                    cols = slice(4 * tp, 4 * tp + 4)
                    act.activation(e0[:, cols], neg_max[:, cols], ACT.Exp).then_inc(exp_done, 1)

                def relu(q):
                    if q == 0:
                        act.wait_ge(ffn_s_in, 2 * b + 2)
                    if begun(HQ * b + q - 1):
                        act.wait_ge(ffn_acc, HQ * b + q - 1)
                    act.activation(ffn_h[q % 2], ffn_s, ACT.Relu, bias=b1c[:, q:q + 1], scale=w1c[:, q:q + 1]) \
                        .then_inc(ffn_relu, 1)

                def value_lines(half):
                    act.wait_ge(v_proj, 2 * n + half + 1)
                    if half == 0:
                        act.activation(vT[:, HALF:HALF + LINE], fill[0][:], ACT.Identity,
                                       accum_out=v_sums[:, 0:1]).then_inc(v_in, 1)
                    else:
                        act.activation(vT[:, HALF + LINE:N], fill[1][:, 0:LINE - HALF], ACT.Identity,
                                       accum_out=v_sums[:, 1:2])
                        act.activation(vT[:, 0:HALF], fill[1][:, LINE - HALF:LINE], ACT.Identity,
                                       accum_out=v_sums[:, 2:3]).then_inc(v_in, 1)

                def qk_high(i):
                    dst, half = (qT[hi][:], i % 2) if i < 2 else (kT[hi][:, HALF:HALF + N], i % 2)
                    due = in_register(act, 4 * n + i + 1)
                    act.wait_ge(qk_proj, 1)
                    act.wait_ge(qk_proj, due)
                    act.activation(dst[:, half * LINE:half * LINE + LINE], fill[QK_BANK[i]][:], ACT.Identity,
                                   bias=bias_qkv[:, Q_ + i // 2, pair]).then_inc(qk_hi, 1)

                def weights_high(u):
                    if begun(4 * j + u - 1):
                        act.wait_ge(pv_done, 4 * j + u - 1)
                    for k in range(2):
                        act.wait_ge(p_T, 8 * j + 2 * u + k + 1)
                        act.activation(pT[u % 2][hi][:, k * LINE:k * LINE + LINE], pT_ps[k][:], ACT.Copy) \
                            .then_inc(pT_hi, 1)

                def output_half(u):
                    h = u % 2
                    act.wait_ge(pv_done, 4 * j + u + 1)
                    act.activation(o_part[h][h * D:h * D + D], o_ps[h][D - h * D:2 * D - h * D], ACT.Copy) \
                        .then_inc(o_half, 1)

                def output_high(half):
                    act.wait_ge(o_summed, 4 * j + 2 * half + 2)
                    if begun(T * o + 4 * half + 4):
                        act.wait_ge(out_done, T * o + 4 * half + 4)
                    act.activation(oT[hi][:, half * LINE:half * LINE + LINE], o_sum[half][:], ACT.Copy) \
                        .then_inc(oT_hi, 1)

                def x_high(items):
                    for i in items:
                        half, k = i // KC, i % KC
                        act.wait_ge(xT_done, T * b + i + 1)
                        act.activation(xT[hi][:, k, half * LINE:half * LINE + LINE], x_banks[i % 4][:], ACT.Copy) \
                            .then_inc(xT_hi, 1)

                if ln:
                    x_high(range(0, 6))
                    value_lines(0)
                    x_high(range(6, T))
                elif proj:
                    value_lines(0)
                if attend:
                    exps(0)
                    exps(1)
                if proj:
                    value_lines(1)
                if not last:
                    split_high(n + 1, V_, v_proj, 2 * n + 2)
                if attend:
                    exps(2)
                if proj:
                    qk_high(0)
                if attend:
                    weights_high(0)
                    exps(3)
                for half in range(2) if ffn_first else ():
                    act.wait_ge(ffn_in, 2 * b + half + 1)
                    act.activation(ffn_s[:, half * LINE:half * LINE + LINE], fill[1 - half][:], ACT.Identity,
                                   bias=ffn_bin[:]).then_inc(ffn_s_in, 1)
                if proj:
                    qk_high(1)
                if attend:
                    weights_high(1)
                    output_half(0)
                if ffn_first or ffn_last:
                    relu(0 if ffn_first else 5)
                if not last:
                    split_high(n + 1, Q_, qk_proj, 4 * n + 2)
                if ln_next:
                    normalise(b + 1, range(0, 4))
                if proj:
                    qk_high(2)
                if attend:
                    weights_high(2)
                    output_half(1)
                if ffn_first or ffn_last:
                    relu(1 if ffn_first else 6)
                if attend:
                    weights_high(3)
                    output_half(2)
                    output_high(0)
                if ffn_first or ffn_last:
                    relu(2 if ffn_first else 7)
                if ln_next:
                    normalise(b + 1, range(4, 7))
                if proj:
                    qk_high(3)
                if attend:
                    act.wait_ge(wo_in, 16 * (j + 1))
                    if begun(T * j):
                        act.wait_ge(out_done, T * j)
                    act.activation(wo[hi][:], wo_raw[:], ACT.Copy).then_inc(wo_hi, 1)
                if attend:
                    output_half(3)
                for i in range(2) if proj else ():
                    act.wait_ge(v_T, 2 * n + i + 1)
                    act.activation(v[:, 4 * i:4 * i + 4, :, hi, :].rearrange("p c h d -> p (c h) d"),
                                   fill[i][:].rearrange("p (c d) -> p c d", d=D), ACT.Copy).then_inc(v_hi, 1)
                if attend:
                    output_high(1)
                if not last:
                    split_high(n + 1, K_, qk_proj, 4 * n + 4)
                if ffn_first:
                    relu(3)
                    relu(4)
                if ln_next:
                    normalise(b + 1, range(7, T))

            run_steps(act, step)

        @block.vector
        def _(dve):
            for part in (hi, lo):
                dve.memset(f32(kT[part][:, 0:HALF]), 0.0).then_inc(dve_set, 1)
                dve.memset(f32(kT[part][:, HALF + N:]), 0.0).then_inc(dve_set, 1)
            dve.memset(b2c[M:2 * M], 0.0).then_inc(dve_set, 1)

            def statistics(b, tiles):
                due = in_register(dve, 16 * (b + 1))
                dve.wait_ge(x_in, 1)
                dve.wait_ge(x_in, due)
                for t in tiles:
                    dve.bn_stats(stats[:, t], acc[:, b % 2, t]).then_inc(ln_stats, 1)

            def mean_and_variance(b):
                due = in_register(dve, T * (b + 1))
                dve.wait_ge(ln_stats, 1)
                dve.wait_ge(ln_stats, due)
                for t in range(T):
                    last = dve.bn_aggr(mean_var[:, t], stats[:, t])
                last.then_inc(ln_agg, 1)

            statistics(0, range(T))
            mean_and_variance(0)
            dve.wait_ge(const_in, 16 * N_CONST)
            for u in range(2):
                dve.tensor_copy(win[hi][:, :, u], win_raw[:]).then_inc(dve_set, 1)
            dve.wait_ge(dve_set, 7)
            for u in range(2):
                dve.tensor_tensor(win[lo][:, :, u], win_raw[:], f32(win[hi][:, :, u]), ALU.subtract) \
                    .then_inc(win_ready, 1)

            def step(n, b, pair, proj=True, attend=True, out_proj=True, ln=False, ln_next=False, ffn_first=False,
                     ffn_last=False, **_):
                j, o = n - 1, n - 2
                parity = (b + 1) % 2 if isinstance(pair, int) and pair < 2 else b % 2

                def mask_scores(tp):
                    due = in_register(dve, 4 * j + tp + 1)
                    dve.wait_ge(scored, 1)
                    dve.wait_ge(scored, due)
                    for h in range(2):
                        for i in range(2):
                            c, t = column(tp, h, i), 2 * tp + i
                            dve.tensor_tensor_reduce(out=probs[:, h, t], in0=score[h][:, i * WIN:i * WIN + WIN],
                                                     in1=mask[:], scale=1.0, scalar=0.0, op0=ALU.mult, op1=ALU.max,
                                                     accum_out=row_max[:, c:c + 1]).then_inc(masked, 1)
                    dve.wait_ge(masked, 16 * j + 4 * tp + 4)
                    cols = slice(4 * tp, 4 * tp + 4)
                    dve.tensor_scalar(neg_max[:, cols], row_max[:, cols], -1.0, None, ALU.mult).then_inc(max_ready, 1)

                def denominators(half):
                    cols = slice(T * half, T * half + T)
                    dve.wait_ge(exp_done, 4 * j + 2 * half + 2)
                    dve.scalar_tensor_tensor(row_l[:, cols], e0[:, cols], float(N - WIN), row_sum[:, cols],
                                             ALU.mult, ALU.add).then_inc(l_ready, 1)
                    dve.wait_ge(l_ready, 2 * j + half + 1)
                    dve.reciprocal(inv_l[:, cols], row_l[:, cols]).then_inc(inv_ready, 1)
                    dve.wait_ge(inv_ready, 2 * j + half + 1)
                    dve.scalar_tensor_tensor(neg_e[:, cols], e0[:, cols], -1.0, inv_l[:, cols],
                                             ALU.mult, ALU.mult).then_inc(norm_ready, 1)

                def add_output(t):
                    dve.wait_ge(out_done, T * o + t + 1)
                    dve.tensor_tensor(acc[:, parity, t], fill[OUT_BANK[t]][:], acc[:, parity, t], ALU.add) \
                        .then_inc(out_added, 1)

                def hidden(q):
                    dve.wait_ge(ffn_relu, HQ * b + q + 1)
                    if q == 0:
                        dve.tensor_scalar(ffn_g, ffn_h[0], w2c[:, 0:1], b2c[:], ALU.mult, ALU.add).then_inc(ffn_acc, 1)
                    else:
                        dve.wait_ge(ffn_acc, HQ * b + q)
                        dve.scalar_tensor_tensor(ffn_g, ffn_h[q % 2], w2c[:, q:q + 1], ffn_g, ALU.mult, ALU.add) \
                            .then_inc(ffn_acc, 1)

                def qk_low(i):
                    part = [(qT[p][:] if i < 2 else kT[p][:, HALF:HALF + N])[:, i % 2 * LINE:i % 2 * LINE + LINE]
                            for p in (hi, lo)]
                    dve.wait_ge(qk_hi, 4 * n + i + 1)
                    dve.scalar_tensor_tensor(part[lo], fill[QK_BANK[i]][:], bias_qkv[:, Q_ + i // 2, pair],
                                             f32(part[hi]), ALU.add, ALU.subtract).then_inc(qk_lo, 1)

                def weights_low(u):
                    for k in range(2):
                        cols = slice(k * LINE, k * LINE + LINE)
                        dve.wait_ge(pT_hi, 8 * j + 2 * u + k + 1)
                        dve.tensor_tensor(pT[u % 2][lo][:, cols], pT_ps[k][:], f32(pT[u % 2][hi][:, cols]),
                                          ALU.subtract).then_inc(pT_lo, 1)

                def output_sum(u):
                    h, half = u % 2, u // 2
                    rows = slice(h * D, h * D + D)
                    dve.wait_ge(o_half, 4 * j + u + 1)
                    dve.wait_ge(v_back_ready, j + 1)
                    if h == 0 and begun(2 * j - 1 + half):
                        dve.wait_ge(oT_lo, 2 * j - 1 + half)
                    dve.scalar_tensor_tensor(o_sum[half][rows], o_ps[h][rows], v_back[rows], o_part[h][rows],
                                             ALU.add, ALU.add).then_inc(o_summed, 1)

                def x_low(items):
                    for i in items:
                        half, k = i // KC, i % KC
                        cols = slice(half * LINE, half * LINE + LINE)
                        dve.wait_ge(xT_hi, T * b + i + 1)
                        dve.tensor_tensor(xT[lo][:, k, cols], x_banks[i % 4][:], f32(xT[hi][:, k, cols]), ALU.subtract) \
                            .then_inc(xT_lo, 1)

                if ln:
                    x_low(range(0, 6))
                if attend:
                    mask_scores(0)
                if ln_next:
                    statistics(b + 1, range(0, 3))
                if out_proj:
                    add_output(0)
                if ffn_last:
                    hidden(3)
                if ln:
                    x_low(range(6, T))
                if attend:
                    mask_scores(1)
                if out_proj:
                    add_output(1)
                if ffn_last:
                    hidden(4)
                if ln_next:
                    statistics(b + 1, range(3, 5))
                if attend:
                    denominators(0)
                    mask_scores(2)
                if out_proj:
                    add_output(2)
                if ln_next:
                    statistics(b + 1, range(5, T))
                    mean_and_variance(b + 1)
                if proj:
                    qk_low(0)
                if out_proj:
                    add_output(3)
                if attend:
                    mask_scores(3)
                if attend:
                    weights_low(0)
                if out_proj and not ffn_first:
                    add_output(4)
                if attend:
                    denominators(1)
                if out_proj and ffn_first:
                    add_output(4)
                if proj:
                    qk_low(1)
                if attend:
                    weights_low(1)
                    output_sum(0)
                if ffn_first or ffn_last:
                    hidden(0 if ffn_first else 5)
                if proj:
                    dve.wait_ge(v_in, 2 * n + 2)
                    dve.tensor_tensor(v_mean[:, 0:1], v_sums[:, 0:1], v_sums[:, 1:2], ALU.add).then_inc(v_stat, 1)
                    dve.wait_ge(v_stat, 3 * n + 1)
                    dve.tensor_tensor(v_mean[:, 1:2], v_mean[:, 0:1], v_sums[:, 2:3], ALU.add).then_inc(v_stat, 1)
                    dve.wait_ge(v_stat, 3 * n + 2)
                    dve.tensor_scalar(v_new[:], v_mean[:, 1:2], 1.0 / N, None, ALU.mult).then_inc(v_stat, 1)
                    dve.wait_ge(v_stat, 3 * n + 3)
                    dve.tensor_scalar(vT[:], vT[:], v_new[:], None, ALU.subtract).then_inc(v_centered, 1)
                if out_proj:
                    add_output(5)
                if proj:
                    qk_low(2)
                if attend:
                    weights_low(2)
                    output_sum(1)
                if out_proj:
                    add_output(6)
                if ffn_first or ffn_last:
                    hidden(1 if ffn_first else 6)
                if attend:
                    weights_low(3)
                    output_sum(2)
                if ffn_first or ffn_last:
                    hidden(2 if ffn_first else 7)
                if out_proj:
                    add_output(7)
                if proj:
                    qk_low(3)
                if attend:
                    output_sum(3)
                for t in range(T) if ffn_last else ():
                    dve.wait_ge(ffn_out, T * b + t + 1)
                    dve.wait_ge(bias_added, T * b + t + 1)
                    dve.tensor_tensor(acc[:, b % 2, t], fill[t % 2][:], acc[:, b % 2, t], ALU.add) \
                        .then_inc(ffn_added, 1)
                for i in range(2) if proj else ():
                    part = [v[:, 4 * i:4 * i + 4, :, p, :].rearrange("p c h d -> p (c h) d") for p in (hi, lo)]
                    dve.wait_ge(v_hi, 2 * n + i + 1)
                    dve.tensor_tensor(part[lo], fill[i][:].rearrange("p (c d) -> p c d", d=D), f32(part[hi]),
                                      ALU.subtract).then_inc(v_lo, 1)
                if proj:
                    if attend:
                        dve.wait_ge(o_summed, 4 * j + 4)
                    dve.tensor_tensor(v_back[:], v_new[:], bias_qkv[:, V_, pair], ALU.add).then_inc(v_back_ready, 1)

            run_steps(dve, step)

        @block.tensor
        def _(pe):
            pe.wait_ge(pool_set, 6)
            pe.wait_ge(dve_set, 5)
            pe.wait_ge(win_ready, 2)
            pe.wait_ge(const_in, 16 * N_CONST)
            pe.transpose(fill[0][:, 0:3 * PAIRS], bias_rows[:], ident[0:3 * PAIRS, 0:3 * PAIRS]).then_inc(bias_T, 1)
            pe.wait_ge(bias_in, 1)

            def step(n, b, pair, proj=True, attend=True, out_proj=True, ln=False, ffn_first=False, ffn_last=False,
                     **_):
                j, o = n - 1, n - 2
                def scores(tp):
                    if tp == 0:
                        pe.wait_ge(qk_lo, 4 * j + 4)
                    if begun(16 * j + 4 * tp):
                        pe.wait_ge(masked, 16 * j + 4 * tp)
                    for i in range(2):
                        t = 2 * tp + i
                        for a, (qp, kp) in enumerate(PASSES):
                            for h in range(2):
                                rows = slice(h * D, h * D + D)
                                last = pe.matmul(score[h][:, i * WIN:i * WIN + WIN], qT[qp][rows, t * P:t * P + P],
                                                 kT[kp][rows, t * P:t * P + WIN], start=(a == 0), stop=(a == 2))
                    last.then_inc(scored, 1)

                def project(i, half, done, dst):
                    pe.wait_ge(w_lo, 3 * n + i + 1)
                    for k in range(KC):
                        for a, (wp, xp) in enumerate(PASSES):
                            last = pe.matmul(dst[:], w[wp][:, i, k], xT[xp][:, k, half * LINE:half * LINE + LINE],
                                             start=(k == 0 and a == 0), stop=(k == KC - 1 and a == 2))
                    last.then_inc(done, 1)

                def project_out(t):
                    if t == 0:
                        pe.wait_ge(wo_lo, o + 1)
                    if t % 4 == 0:
                        pe.wait_ge(oT_lo, 2 * o + t // 4 + 1)
                    dst = fill[OUT_BANK[t]]
                    for a, (op, wp) in enumerate(PASSES):
                        last = pe.matmul(dst[:], oT[op][:, t * P:t * P + P], wo[wp][:], start=(a == 0), stop=(a == 2))
                    last.then_inc(out_done, 1)

                def transpose_x(i):
                    half, k = i // KC, i % KC
                    pe.wait_ge(xn_ready, T * b + 4 * half + 4)
                    for t in tiles_of(half):
                        last = pe.transpose(x_banks[i % 4][:, t % 4 * P:t % 4 * P + P], xn[:, t, k * P:k * P + P], ident[:])
                    last.then_inc(xT_done, 1)

                def network_in(half):
                    for k in range(KC):
                        for a, (wp, xp) in enumerate(PASSES):
                            last = pe.matmul(fill[1 - half][:], win[wp][:, k].rearrange("p u m -> p (u m)"),
                                             xT[xp][:, k, half * LINE:half * LINE + LINE],
                                             start=(k == 0 and a == 0), stop=(k == KC - 1 and a == 2))
                    last.then_inc(ffn_in, 1)

                def transpose_values(i):
                    for c in range(4):
                        last = pe.transpose(fill[i][:, c * P:c * P + P], vT[:, (4 * i + c) * P:(4 * i + c + 1) * P],
                                            ident[:])
                    last.then_inc(v_T, 1)

                def transpose_weights(u):
                    half, h = u // 2, u % 2
                    pe.wait_ge(normed, 16 * j + 4 * u + 4)
                    for i in range(8):
                        t, c, k = 4 * half + i // 2, i % 2, i // 4
                        if i % 4 == 0 and begun(8 * j + 2 * u + k - 1):
                            pe.wait_ge(pT_lo, 8 * j + 2 * u + k - 1)
                        last = pe.transpose(pT_ps[k][:, i % 4 * P:i % 4 * P + P], probs[:, h, t, c * P:c * P + P],
                                            ident[:])
                        if i % 4 == 3:
                            last.then_inc(p_T, 1)

                def weigh_values(u):
                    half, h = u // 2, u % 2
                    pe.wait_ge(pT_lo, 8 * j + 2 * u + 2)
                    if u == 0:
                        pe.wait_ge(v_lo, 2 * j + 2)
                    if begun(4 * j + u - 1):
                        pe.wait_ge(o_summed, 4 * j + u - 1)
                    for k in range(5):
                        first, end = max(2 * k - 1, 0), min(2 * k + 1, 8)
                        q0 = max(k - 1, 0) * P
                        for part in (hi, lo):
                            last = pe.matmul(o_ps[h][:, q0:q0 + (end - first) * P],
                                             v[:, (4 * half + k) % T, h].rearrange("p a d -> p (a d)"),
                                             pT[h][part][:, first * P:end * P], start=(k == 0 and part == hi),
                                             stop=(k == 4 and part == lo), skip_group_check=True)
                    last.then_inc(pv_done, 1)

                if ln:
                    transpose_x(0)
                    transpose_x(1)
                if attend:
                    scores(0)
                if ln:
                    for i in (2, 3):
                        if begun(2 * n - 3 + i):
                            pe.wait_ge(v_lo, 2 * n - 3 + i)
                        transpose_x(i)
                    for i in (4, 5):
                        pe.wait_ge(xT_lo, T * b + i - 3)
                        transpose_x(i)
                if proj:
                    if ln:
                        pe.wait_ge(xT_lo, T * b + KC)
                    else:
                        pe.wait_ge(v_lo, 2 * n - 1)
                    project(V_, 0, v_proj, fill[0])
                if out_proj:
                    if not attend:
                        pe.wait_ge(out_added, T * o)
                    elif not ln:
                        pe.wait_ge(v_lo, 2 * n)
                    project_out(0)
                if ln:
                    pe.wait_ge(v_in, 2 * n + 1)
                    transpose_x(6)
                    if out_proj:
                        pe.wait_ge(out_added, T * o + 1)
                    transpose_x(7)
                if attend:
                    scores(1)
                if ln:
                    pe.wait_ge(xT_lo, T * b + T)
                if out_proj:
                    if proj and not ln:
                        pe.wait_ge(v_in, 2 * n + 1)
                    elif attend and not proj:
                        pe.wait_ge(v_lo, 2 * n - 1)
                    project_out(1)
                if proj:
                    if out_proj and not ln:
                        pe.wait_ge(out_added, T * o + 1)
                    elif not ln:
                        pe.wait_ge(v_lo, 2 * n)
                    project(V_, 1, v_proj, fill[1])
                if attend:
                    scores(2)
                if out_proj:
                    pe.wait_ge(out_added, T * o + 2)
                    project_out(2)
                if proj:
                    pe.wait_ge(v_in, 2 * n + 2)
                    project(Q_, 0, qk_proj, fill[QK_BANK[0]])
                if attend:
                    scores(3)
                if out_proj:
                    pe.wait_ge(out_added, T * o + 3)
                    project_out(3)
                if attend:
                    transpose_weights(0)
                if ffn_first:
                    pe.wait_ge(qk_lo, 4 * n + 1)
                    network_in(0)
                    if out_proj:
                        pe.wait_ge(out_added, T * o + 4)
                    network_in(1)
                if out_proj:
                    if ffn_first:
                        pe.wait_ge(ffn_s_in, 2 * b + 1)
                    elif proj:
                        pe.wait_ge(qk_lo, 4 * n + 1)
                    project_out(4)
                if proj:
                    if ffn_first:
                        pe.wait_ge(ffn_s_in, 2 * b + 2)
                    elif out_proj:
                        pe.wait_ge(out_added, T * o + 4)
                    else:
                        pe.wait_ge(v_in, 2 * n + 1)
                    project(Q_, 1, qk_proj, fill[QK_BANK[1]])
                if attend:
                    transpose_weights(1)
                    weigh_values(0)
                if proj:
                    if out_proj:
                        pe.wait_ge(out_added, T * o + 5)
                    else:
                        pe.wait_ge(qk_lo, 4 * n + 1)
                    project(K_, 0, qk_proj, fill[QK_BANK[2]])
                if out_proj:
                    if proj:
                        pe.wait_ge(qk_lo, 4 * n + 2)
                    else:
                        pe.wait_ge(out_added, T * o + 4)
                    project_out(5)
                if attend:
                    transpose_weights(2)
                    weigh_values(1)
                if out_proj:
                    pe.wait_ge(out_added, T * o + 6)
                    project_out(6)
                if attend:
                    transpose_weights(3)
                    weigh_values(2)
                if proj:
                    pe.wait_ge(qk_lo, 4 * n + 3)
                    project(K_, 1, qk_proj, fill[QK_BANK[3]])
                if out_proj:
                    pe.wait_ge(out_added, T * o + 7)
                    project_out(7)
                if attend:
                    weigh_values(3)
                if ffn_last:
                    pe.wait_ge(ffn_acc, HQ * b + HQ)
                for t in range(T) if ffn_last else ():
                    if t == 0 and out_proj:
                        pe.wait_ge(out_added, T * o + T)
                    elif t == 1:
                        pe.wait_ge(qk_lo, 4 * n + 4)
                    elif t > 1:
                        pe.wait_ge(ffn_added, T * b + t - 1)
                    pe.matmul(fill[t % 2][:], ffn_g[:, t * P:t * P + P], wout[:], start=True, stop=True).then_inc(ffn_out, 1)
                if proj:
                    pe.wait_ge(v_centered, n + 1)
                    if ffn_last:
                        pe.wait_ge(ffn_added, T * b + T - 1)
                    elif out_proj:
                        pe.wait_ge(out_added, T * o + T)
                    transpose_values(0)
                    if ffn_last:
                        pe.wait_ge(ffn_added, T * b + T)
                    else:
                        pe.wait_ge(qk_lo, 4 * n + 4)
                    transpose_values(1)

            run_steps(pe, step)


_INS = ["L0_attn_x", "L0_attn_Wq", "L0_attn_bq", "L0_attn_Wk", "L0_attn_bk", "L0_attn_Wv", "L0_attn_bv", "L0_attn_Wo",
        "L0_attn_bo", "L0_ffn_Win", "L0_ffn_bin_", "L0_ffn_W1", "L0_ffn_b1", "L0_ffn_W2", "L0_ffn_b2", "L0_ffn_Wout",
        "L0_ffn_bout"]


def kernel(**inputs):
    import numpy as np
    import concourse.bacc as bacc
    from concourse.bass_utils import run_bass_kernel_spmd

    nc = bacc.Bacc("TRN2", target_bir_lowering=False, num_devices=1)
    arrays, args = {}, []
    for name in _INS:
        a = np.ascontiguousarray(inputs[name])
        arrays[f"in_{name}"] = a
        args.append(nc.dram_tensor(f"in_{name}", a.shape, mybir.dt.from_np(a.dtype), kind="ExternalInput").ap())
    shape = inputs["L0_attn_x"].shape
    args.append(nc.dram_tensor("out_x", shape, F32, kind="ExternalOutput").ap())
    band_attention_ffn(nc, *args)
    return run_bass_kernel_spmd(nc, [arrays], core_ids=[0]).results[0]["out_x"]
```

```python
from contextlib import ExitStack

import concourse.bass as bass
from concourse import mybir

F32 = mybir.dt.float32
F32R = mybir.dt.float32r
ALU = mybir.AluOpType
ACT = mybir.ActivationFunctionType

P = 128


def begun(count):
    return not isinstance(count, int) or count > 0


def in_register(engine, count):
    return count if isinstance(count, int) else engine.to_reg(count)


def band_attention_ffn(nc, x, Wq, bq, Wk, bk, Wv, bv, Wo, bo, Win, bin_, W1, b1, W2, b2, Wout, bout, out):
    B, N, E = x.shape
    HD = Wq.shape[1]
    D = 64
    PAIRS = HD // P
    M, INNER = W1.shape
    T = N // P
    KC = E // P
    HALF = 64
    WIN = 2 * P
    LINE = N // 2
    HQ = INNER // 2
    EPS = 1e-5
    assert (E, N, HD, M, B) == (4 * P, 8 * P, 1024, 64, 8) and HALF + P <= WIN

    with ExitStack() as ctx:
        def sb(name, shape, dt=F32):
            return ctx.enter_context(nc.sbuf_tensor(name, shape, dt))

        def bank(name):
            return ctx.enter_context(nc.psum_tensor(name, [P, 512], F32))

        def sem(name):
            return ctx.enter_context(nc.semaphore(name))

        acc = sb("acc", [P, 2, T, E])
        xn = sb("xn", [P, T, E])
        ffn = xn[:].rearrange("p t e -> p (t e)")
        ffn_s, ffn_g = ffn[:, 0:N], ffn[:, N:2 * N]
        ffn_h = [ffn[:, 2 * N:3 * N], ffn[:, 3 * N:4 * N]]
        ffn_part = ffn_h[0]
        ffn_g_parts = [sb(f"ffn_g_{part}", [P, N], F32R) for part in ("hi", "lo")]
        xT = [sb(f"xT_{part}", [P, KC, N], F32R) for part in ("hi", "lo")]
        w_raw = sb("w_raw", [P, 3, KC, P])
        w = [sb(f"w_{part}", [P, 3, KC, P], F32R) for part in ("hi", "lo")]
        wo_raw = sb("wo_raw", [P, E])
        wo = [sb(f"wo_{part}", [P, E], F32R) for part in ("hi", "lo")]
        qT = [sb(f"qT_{part}", [P, N], F32R) for part in ("hi", "lo")]
        kT = [sb(f"kT_{part}", [P, N + 2 * HALF], F32R) for part in ("hi", "lo")]
        vT = sb("vT", [P, N])
        v = sb("v", [P, T, 2, 2, D], F32R)
        probs = sb("probs", [P, 2, T, WIN])
        pT = [[sb(f"pT{i}_{part}", [P, 2 * LINE], F32R) for part in ("hi", "lo")] for i in range(2)]
        o_part = [sb(f"o_part{i}", [P, LINE]) for i in range(2)]
        o_sum = [sb(f"o_sum{i}", [P, LINE]) for i in range(2)]
        oT = [sb(f"oT_{part}", [P, N], F32R) for part in ("hi", "lo")]
        mask = sb("mask", [P, WIN])
        ident = sb("ident", [P, P])
        bias_row = sb("bias_row", [P, E])
        bias_2 = sb("bias_2", [P, E])
        bias_rows = sb("bias_rows", [3 * PAIRS, P])
        bias_qkv = sb("bias_qkv", [P, 3, PAIRS, 1])
        win_raw = sb("win_raw", [P, KC, M])
        win = sb("win", [P, KC, 2, M], F32R)
        wout_raw = sb("wout_raw", [P, E])
        wout = [sb(f"wout_{part}", [P, E], F32R) for part in ("hi", "lo")]
        ffn_bin = sb("ffn_bin", [P, 1])
        w1c, b1c, w2c = sb("w1c", [P, HQ]), sb("b1c", [P, HQ]), sb("w2c", [P, HQ])
        b2c = sb("b2c", [P, 1])
        stats = sb("stats", [P, T, 6])
        mean_var = sb("mean_var", [P, T, 2])
        minus_half = sb("minus_half", [P, T])
        var_eps, rstd = sb("var_eps", [P, T]), sb("rstd", [P, T])
        mean_rstd, shift = sb("mean_rstd", [P, T]), sb("shift", [P, T])
        row_max, neg_max, row_sum, e0 = (sb(s, [P, 2 * T]) for s in ("row_max", "neg_max", "row_sum", "e0"))
        row_l, inv_l, neg_e = (sb(s, [P, 2 * T]) for s in ("row_l", "inv_l", "neg_e"))
        v_sums, v_mean, v_new = sb("v_sums", [P, 3]), sb("v_mean", [P, 2]), sb("v_new", [P, 1])
        v_back = sb("v_back", [P, 1])

        fill = [bank("fill0"), bank("fill1")]
        score = [bank("score0"), bank("score1")]
        pT_ps = [bank("pT_ps0"), bank("pT_ps1")]
        o_ps = [bank("o_ps0"), bank("o_ps1")]
        ffn_banks = pT_ps + fill

        const_in = sem("const_in")
        bias_T, bias_in = sem("bias_T"), sem("bias_in")
        x_first, x_in, wo_in = sem("x_first"), sem("x_in"), sem("wo_in")
        w_in = [sem(f"w_in_{s}") for s in "vqk"]
        stored = sem("stored")
        pool_set, dve_set, win_ready = sem("pool_set"), sem("dve_set"), sem("win_ready")
        ln_stats, ln_agg, ln_small, xn_ready = sem("ln_stats"), sem("ln_agg"), sem("ln_small"), sem("xn_ready")
        xT_done, xT_hi, xT_lo = sem("xT_done"), sem("xT_hi"), sem("xT_lo")
        w_hi, w_lo = sem("w_hi"), sem("w_lo")
        wo_hi, wo_lo = sem("wo_hi"), sem("wo_lo")
        v_proj, v_in, v_stat, v_centered = sem("v_proj"), sem("v_in"), sem("v_stat"), sem("v_centered")
        v_back_ready = sem("v_back_ready")
        v_T, v_hi, v_lo = sem("v_T"), sem("v_hi"), sem("v_lo")
        qk_proj, qk_hi, qk_lo = sem("qk_proj"), sem("qk_hi"), sem("qk_lo")
        scored, masked, max_ready = sem("scored"), sem("masked"), sem("max_ready")
        exp_done, l_ready, inv_ready, norm_ready = sem("exp_done"), sem("l_ready"), sem("inv_ready"), sem("norm_ready")
        normed, p_T, pT_hi, pT_lo = sem("normed"), sem("p_T"), sem("pT_hi"), sem("pT_lo")
        pv_done, o_half, o_summed, oT_hi, oT_lo = (sem(s) for s in ("pv_done", "o_half", "o_summed", "oT_hi", "oT_lo"))
        out_done, out_added = sem("out_done"), sem("out_added")
        bias_added = sem("bias_added")
        ffn_in, ffn_half, ffn_s_in = sem("ffn_in"), sem("ffn_half"), sem("ffn_s_in")
        ffn_relu, ffn_acc, ffn_g_hi, ffn_g_lo = sem("ffn_relu"), sem("ffn_acc"), sem("ffn_g_hi"), sem("ffn_g_lo")
        ffn_out, ffn_added = sem("ffn_out"), sem("ffn_added")

        hi, lo = 0, 1
        PASSES = [(hi, hi), (hi, lo), (lo, hi)]
        V_, Q_, K_ = 0, 1, 2
        OUT_BANK = (1, 0, 0, 0, 1, 0, 0, 0)
        QK_BANK = (1, 0, 1, 1)
        x_d = x.rearrange("b (t p) e -> b p t e", p=P)
        out_d = out.rearrange("b (t p) e -> b p t e", p=P)
        w_d = [m.rearrange("(k p) (h c) -> h p k c", p=P, c=P) for m in (Wv, Wq, Wk)]
        wo_d = Wo.rearrange("(h p) e -> h p e", p=P)
        N_CONST = 3 + 1 + 2 * 5 + 1 + 2

        def f32(a):
            return a.bitcast(F32)

        def column(tp, h, i):
            return 4 * tp + 2 * h + i

        def tiles_of(half):
            return range(4 * half, 4 * half + 4)

        def run_steps(engine, step):
            def middle(b):
                with engine.Fori(2, PAIRS - 2) as pair:
                    step(b * PAIRS + pair, b, pair, after_ffn=True)

            step(0, 0, 0, attend=False, out_proj=False, ln=True, ffn_first=True)
            step(1, 0, 1, out_proj=False, ffn_last=True)
            middle(0)
            with engine.Fori(1, B) as b:
                step(b * PAIRS - 2, b - 1, PAIRS - 2, stats_next=True)
                step(b * PAIRS - 1, b - 1, PAIRS - 1, ln_next=True)
                step(b * PAIRS, b, 0, ln=True, ffn_first=True)
                step(b * PAIRS + 1, b, 1, ffn_last=True)
                middle(b)
            step(B * PAIRS - 2, B - 1, PAIRS - 2)
            step(B * PAIRS - 1, B - 1, PAIRS - 1, last=True)
            step(B * PAIRS, B, 0, proj=False, last=True)
            step(B * PAIRS + 1, B, 1, proj=False, attend=False, last=True)

        block = ctx.enter_context(nc.Block())

        @block.sync
        def _(sp):
            def load_weights(n, pair):
                for i in range(3):
                    if begun(3 * (n - 1) + i + 1):
                        sp.wait_ge(w_lo, 3 * (n - 1) + i + 1)
                    sp.dma_start(w_raw[:, i], w_d[i][pair]).then_inc(w_in[i], 16)

            def load_output_weights(n, pair):
                if begun(n):
                    sp.wait_ge(wo_lo, n)
                sp.dma_start(wo_raw[:], wo_d[pair]).then_inc(wo_in, 16)

            def store(b):
                sp.wait_ge(out_added, (b + 1) * PAIRS * T)
                sp.dma_start(out_d[b], acc[:, b % 2]).then_inc(stored, 16)

            sp.dma_start(acc[:, 0, 0:4], x_d[0][:, 0:4]).then_inc(x_first, 16)
            sp.dma_start(acc[:, 0, 4:T], x_d[0][:, 4:T]).then_inc(x_in, 16)
            load_weights(0, 0)
            for i, m in enumerate((bv, bq, bk)):
                rows = slice(i * PAIRS, i * PAIRS + PAIRS)
                sp.dma_start(bias_rows[rows], m.rearrange("(h p) -> h p", p=P)).then_inc(const_in, 16)
            sp.dma_start(win_raw[:], Win.rearrange("(k p) m -> p k m", p=P)).then_inc(const_in, 16)
            for u in range(2):
                rows = slice(u * M, u * M + M)
                sp.dma_start(ffn_bin[rows], bin_.rearrange("(m o) -> m o", o=1)).then_inc(const_in, 16)
                for dst, src in ((w1c, W1), (b1c, b1), (w2c, W2)):
                    sp.dma_start(dst[rows], src[:, u * HQ:u * HQ + HQ]).then_inc(const_in, 16)
                sp.dma_start(wout_raw[rows], Wout).then_inc(const_in, 16)
            sp.dma_start(b2c[0:M], b2.rearrange("(m o) -> m o", o=1)).then_inc(const_in, 16)
            sp.dma_start(bias_row[:], bo.rearrange("(o e) -> o e", o=1).broadcast_to([P, E])).then_inc(const_in, 16)
            sp.dma_start(bias_2[:], bout.rearrange("(o e) -> o e", o=1).broadcast_to([P, E])).then_inc(const_in, 16)
            sp.wait_ge(x_in, 16)
            sp.dma_start(acc[:, 1], x_d[1]).then_inc(x_in, 16)

            def step(n, b, pair, proj=True, ffn_last=False, last=False, **_):
                if not last:
                    load_weights(n + 1, (pair + 1) if not isinstance(pair, int) else (pair + 1) % PAIRS)
                if proj:
                    load_output_weights(n, pair)
                if ffn_last and not isinstance(b, int):
                    store(b - 1)
                    sp.wait_ge(stored, 16 * b)
                    sp.dma_start(acc[:, (b + 1) % 2], x_d[(b + 1) % B]).then_inc(x_in, 16)

            run_steps(sp, step)
            for tiles in (slice(0, 4), slice(4, T)):
                sp.wait_ge(out_added, B * PAIRS * T - T + tiles.stop)
                sp.dma_start(out_d[B - 1][:, tiles], acc[:, (B - 1) % 2, tiles]).then_inc(stored, 16)
            sp.wait_ge(stored, 16 * (B + 1))
            sp.wait_ge(x_in, 16 * (B + 1))

        @block.gpsimd
        def _(pool):
            pool.memset(ident[:], 0.0).then_inc(pool_set, 1)
            pool.memset(mask[:], 1.0).then_inc(pool_set, 1)
            pool.memset(minus_half[:], -0.5).then_inc(pool_set, 1)
            pool.wait_ge(pool_set, 2)
            pool.affine_select(out=ident[:], in_=ident[:], compare_op=ALU.not_equal, fill=1.0, base=0,
                               pattern=[[-1, P]], channel_multiplier=1).then_inc(pool_set, 1)
            pool.affine_select(out=mask[:], in_=mask[:], compare_op=ALU.is_ge, fill=0.0, base=0,
                               pattern=[[1, WIN]], channel_multiplier=-1).then_inc(pool_set, 1)
            pool.wait_ge(pool_set, 5)
            pool.affine_select(out=mask[:], in_=mask[:], compare_op=ALU.is_ge, fill=0.0, base=2 * HALF,
                               pattern=[[-1, WIN]], channel_multiplier=1).then_inc(pool_set, 1)

            def layer_norm(b):
                due = in_register(pool, b + 1)
                pool.wait_ge(ln_agg, 1)
                pool.wait_ge(ln_agg, due)
                pool.tensor_scalar(var_eps[:], mean_var[:, :, 1], EPS, None, ALU.add).then_inc(ln_small, 1)
                pool.wait_ge(ln_small, 4 * b + 1)
                pool.tensor_tensor(rstd[:], var_eps[:], minus_half[:], ALU.pow).then_inc(ln_small, 1)
                pool.wait_ge(ln_small, 4 * b + 2)
                pool.tensor_tensor(mean_rstd[:], mean_var[:, :, 0], rstd[:], ALU.mult).then_inc(ln_small, 1)
                due = in_register(pool, 4 * b + 3)
                pool.wait_ge(ln_small, 1)
                pool.wait_ge(ln_small, due)
                pool.tensor_scalar(shift[:], mean_rstd[:], -1.0, 0.0, ALU.mult, ALU.add).then_inc(ln_small, 1)

            def split_low(n, i):
                pool.wait_ge(w_hi, 3 * n + i + 1)
                pool.tensor_tensor(w[lo][:, i], w_raw[:, i], f32(w[hi][:, i]), ALU.subtract).then_inc(w_lo, 1)

            split_low(0, V_)
            layer_norm(0)
            split_low(0, Q_)
            split_low(0, K_)
            pool.wait_ge(const_in, 16 * N_CONST)
            pool.tensor_tensor(bias_row[:], bias_row[:], bias_2[:], ALU.add).then_inc(pool_set, 1)
            pool.wait_ge(pool_set, 7)

            def step(n, b, pair, attend=True, stats_next=False, ffn_first=False, ffn_last=False, last=False, **_):
                j = n - 1

                def normalise_weights(half):
                    due = in_register(pool, 2 * j + half + 1)
                    pool.wait_ge(norm_ready, 1)
                    pool.wait_ge(norm_ready, due)
                    for h in range(2):
                        for t in tiles_of(half):
                            c = column(t // 2, h, t % 2)
                            pool.tensor_scalar(probs[:, h, t], probs[:, h, t], inv_l[:, c:c + 1], neg_e[:, c:c + 1],
                                               ALU.mult, ALU.add).then_inc(normed, 1)

                def output_low(half):
                    cols = slice(half * LINE, half * LINE + LINE)
                    pool.wait_ge(oT_hi, 2 * j + half + 1)
                    pool.tensor_tensor(oT[lo][:, cols], o_sum[half][:], f32(oT[hi][:, cols]), ALU.subtract) \
                        .then_inc(oT_lo, 1)

                def add_biases(tiles):
                    pool.wait_ge(xn_ready, T * b + T)
                    for t in tiles:
                        pool.tensor_tensor(acc[:, b % 2, t], acc[:, b % 2, t], bias_row[:], ALU.add) \
                            .then_inc(bias_added, 1)

                if attend:
                    normalise_weights(0)
                if not last:
                    split_low(n + 1, V_)
                if stats_next:
                    layer_norm(b + 1)
                if attend:
                    normalise_weights(1)
                if ffn_first or ffn_last:
                    add_biases([0, 1] if ffn_first else [4, 5])
                if not last:
                    split_low(n + 1, Q_)
                if attend:
                    output_low(0)
                if ffn_first or ffn_last:
                    add_biases([2, 3] if ffn_first else [6, 7])
                if attend:
                    pool.wait_ge(wo_hi, j + 1)
                    pool.tensor_tensor(wo[lo][:], wo_raw[:], f32(wo[hi][:]), ALU.subtract).then_inc(wo_lo, 1)
                    output_low(1)
                if not last:
                    split_low(n + 1, K_)

            run_steps(pool, step)

        @block.scalar
        def _(act):
            def split_high(n, i, used, count):
                act.wait_ge(w_in[i], 16 * (n + 1))
                if begun(count):
                    act.wait_ge(used, count)
                act.activation(w[hi][:, i], w_raw[:, i], ACT.Copy).then_inc(w_hi, 1)

            def normalise(b, tiles):
                due = in_register(act, 4 * b + 4)
                act.wait_ge(ln_small, 1)
                act.wait_ge(ln_small, due)
                if begun(T * b):
                    due = in_register(act, T * b)
                    act.wait_ge(ffn_out, 1)
                    act.wait_ge(ffn_out, due)
                for t in tiles:
                    act.activation(xn[:, t], acc[:, b % 2, t], ACT.Identity, bias=shift[:, t:t + 1],
                                   scale=rstd[:, t:t + 1]).then_inc(xn_ready, 1)

            for i in range(3):
                split_high(0, i, v_proj, 0)
            normalise(0, tiles_of(0))
            act.wait_ge(const_in, 16 * N_CONST)
            act.wait_ge(bias_T, 1)
            act.activation(bias_qkv[:].rearrange("p i h o -> p (i h o)"), score[0][:, 0:3 * PAIRS], ACT.Copy) \
                .then_inc(bias_in, 1)
            normalise(0, tiles_of(1))
            act.wait_ge(bias_in, 1)

            def step(n, b, pair, proj=True, attend=True, ln=False, ln_next=False, ffn_first=False, ffn_last=False,
                     last=False, **_):
                j, o = n - 1, n - 2

                def exps(tp):
                    act.wait_ge(max_ready, 4 * j + tp + 1)
                    for h in range(2):
                        for i in range(2):
                            c, t = column(tp, h, i), 2 * tp + i
                            act.activation(probs[:, h, t], probs[:, h, t], ACT.Exp, bias=neg_max[:, c:c + 1],
                                           accum_out=row_sum[:, c:c + 1])
                    cols = slice(4 * tp, 4 * tp + 4)
                    act.activation(e0[:, cols], neg_max[:, cols], ACT.Exp).then_inc(exp_done, 1)

                def relu(q):
                    if q == 0:
                        act.wait_ge(ffn_s_in, 2 * b + 2)
                    if begun(HQ * b + q - 1):
                        act.wait_ge(ffn_acc, HQ * b + q - 1)
                    act.activation(ffn_h[q % 2], ffn_s, ACT.Relu, bias=b1c[:, q:q + 1], scale=w1c[:, q:q + 1]) \
                        .then_inc(ffn_relu, 1)

                def value_lines(half):
                    act.wait_ge(v_proj, 2 * n + half + 1)
                    if half == 0:
                        act.activation(vT[:, HALF:HALF + LINE], fill[0][:], ACT.Identity,
                                       accum_out=v_sums[:, 0:1]).then_inc(v_in, 1)
                    else:
                        act.activation(vT[:, HALF + LINE:N], fill[1][:, 0:LINE - HALF], ACT.Identity,
                                       accum_out=v_sums[:, 1:2])
                        act.activation(vT[:, 0:HALF], fill[1][:, LINE - HALF:LINE], ACT.Identity,
                                       accum_out=v_sums[:, 2:3]).then_inc(v_in, 1)

                def qk_high(i):
                    dst, half = (qT[hi][:], i % 2) if i < 2 else (kT[hi][:, HALF:HALF + N], i % 2)
                    due = in_register(act, 4 * n + i + 1)
                    act.wait_ge(qk_proj, 1)
                    act.wait_ge(qk_proj, due)
                    act.activation(dst[:, half * LINE:half * LINE + LINE], fill[QK_BANK[i]][:], ACT.Identity,
                                   bias=bias_qkv[:, Q_ + i // 2, pair]).then_inc(qk_hi, 1)

                def weights_high(u):
                    if begun(4 * j + u - 1):
                        act.wait_ge(pv_done, 4 * j + u - 1)
                    for k in range(2):
                        act.wait_ge(p_T, 8 * j + 2 * u + k + 1)
                        act.activation(pT[u % 2][hi][:, k * LINE:k * LINE + LINE], pT_ps[k][:], ACT.Copy) \
                            .then_inc(pT_hi, 1)

                def output_half(u):
                    h = u % 2
                    act.wait_ge(pv_done, 4 * j + u + 1)
                    act.activation(o_part[h][h * D:h * D + D], o_ps[h][D - h * D:2 * D - h * D], ACT.Copy) \
                        .then_inc(o_half, 1)

                def output_high(half, j=j):
                    act.wait_ge(o_summed, 4 * j + 2 * half + 2)
                    if begun(T * (j - 1) + 4 * half + 4):
                        act.wait_ge(out_done, T * (j - 1) + 4 * half + 4)
                    act.activation(oT[hi][:, half * LINE:half * LINE + LINE], o_sum[half][:], ACT.Copy) \
                        .then_inc(oT_hi, 1)

                def values_high(i):
                    act.wait_ge(v_T, 2 * n + i + 1)
                    act.activation(v[:, 4 * i:4 * i + 4, :, hi, :].rearrange("p c h d -> p (c h) d"),
                                   fill[i][:].rearrange("p (c d) -> p c d", d=D), ACT.Copy).then_inc(v_hi, 1)

                def x_high(b, items):
                    for i in items:
                        half, k = i // KC, i % KC
                        act.wait_ge(xT_done, T * b + i + 1)
                        act.activation(xT[hi][:, k, half * LINE:half * LINE + LINE], pT_ps[i % 2][:], ACT.Copy) \
                            .then_inc(xT_hi, 1)

                if ln:
                    x_high(b, range(4 if attend else 0, 6))
                    if attend:
                        output_high(1, j - 1)
                        split_high(n, K_, qk_proj, 4 * n)
                    value_lines(0)
                    x_high(b, range(6, T))
                elif proj:
                    value_lines(0)
                if attend:
                    exps(0)
                if ffn_last:
                    relu(4)
                if ln_next:
                    normalise(b + 1, range(0, 2))
                if attend:
                    exps(1)
                if proj:
                    value_lines(1)
                if not last:
                    split_high(n + 1, V_, v_proj, 2 * n + 2)
                if ffn_last:
                    relu(5)
                if ln_next:
                    normalise(b + 1, range(2, 4))
                if attend:
                    exps(2)
                if proj:
                    qk_high(0)
                if attend:
                    weights_high(0)
                for half in range(2) if ffn_first else ():
                    act.wait_ge(ffn_in, 2 * b + half + 1)
                    for rows, other in ((slice(0, M), slice(M, P)), (slice(M, P), slice(0, M))):
                        copied = act.activation(ffn_part[rows, half * LINE:half * LINE + LINE],
                                                fill[1 - half][other], ACT.Copy)
                    copied.then_inc(ffn_half, 1)
                if attend:
                    exps(3)
                if proj and not ffn_first:
                    qk_high(1)
                if attend:
                    weights_high(1)
                    output_half(0)
                if proj and ffn_first:
                    qk_high(1)
                if ffn_first or ffn_last:
                    relu(0 if ffn_first else 6)
                if not last:
                    split_high(n + 1, Q_, qk_proj, 4 * n + 2)
                if ln_next:
                    normalise(b + 1, range(4, 6))
                if proj:
                    qk_high(2)
                if attend:
                    weights_high(2)
                    output_half(1)
                if ffn_first or ffn_last:
                    relu(1 if ffn_first else 7)
                if attend:
                    weights_high(3)
                    output_high(0)
                if ffn_first:
                    relu(2)
                if ffn_last:
                    act.wait_ge(ffn_acc, HQ * b + HQ)
                    act.activation(ffn_g_parts[hi][:], ffn_g, ACT.Copy).then_inc(ffn_g_hi, 1)
                if ln_next:
                    normalise(b + 1, range(6, T))
                if proj:
                    qk_high(3)
                if ln_next:
                    x_high(b + 1, range(0, 2))
                if attend:
                    act.wait_ge(wo_in, 16 * (j + 1))
                    if begun(T * j):
                        act.wait_ge(out_done, T * j)
                    act.activation(wo[hi][:], wo_raw[:], ACT.Copy).then_inc(wo_hi, 1)
                    output_half(2)
                if ln_next:
                    x_high(b + 1, range(2, 4))
                if proj:
                    values_high(0)
                if attend:
                    output_half(3)
                if proj:
                    values_high(1)
                if attend and not ln_next:
                    output_high(1)
                if not last and not ln_next:
                    split_high(n + 1, K_, qk_proj, 4 * n + 4)
                if ffn_first:
                    relu(3)

            run_steps(act, step)

        @block.vector
        def _(dve):
            for part in (hi, lo):
                dve.memset(f32(kT[part][:, 0:HALF]), 0.0).then_inc(dve_set, 1)
                dve.memset(f32(kT[part][:, HALF + N:]), 0.0).then_inc(dve_set, 1)
            dve.memset(b2c[M:2 * M], 0.0).then_inc(dve_set, 1)

            def statistics(b, tiles):
                due = in_register(dve, 16 * (b + 1))
                dve.wait_ge(x_in, 1)
                dve.wait_ge(x_in, due)
                for t in tiles:
                    dve.bn_stats(stats[:, t], acc[:, b % 2, t]).then_inc(ln_stats, 1)

            def mean_and_variance(b):
                due = in_register(dve, T * (b + 1))
                dve.wait_ge(ln_stats, 1)
                dve.wait_ge(ln_stats, due)
                for t in range(T):
                    last = dve.bn_aggr(mean_var[:, t], stats[:, t])
                last.then_inc(ln_agg, 1)

            dve.wait_ge(x_first, 16)
            for t in tiles_of(0):
                dve.bn_stats(stats[:, t], acc[:, 0, t]).then_inc(ln_stats, 1)
            statistics(0, tiles_of(1))
            mean_and_variance(0)
            dve.wait_ge(const_in, 16 * N_CONST)
            dve.tensor_copy(win[:, :, hi], win_raw[:]).then_inc(dve_set, 1)
            dve.tensor_copy(wout[hi][:], wout_raw[:]).then_inc(dve_set, 1)
            dve.wait_ge(dve_set, 7)
            dve.tensor_tensor(win[:, :, lo], win_raw[:], f32(win[:, :, hi]), ALU.subtract).then_inc(win_ready, 1)
            dve.tensor_tensor(wout[lo][:], wout_raw[:], f32(wout[hi][:]), ALU.subtract).then_inc(win_ready, 1)

            def step(n, b, pair, proj=True, attend=True, out_proj=True, ln=False, ln_next=False, stats_next=False,
                     ffn_first=False, ffn_last=False, **_):
                j, o = n - 1, n - 2
                parity = (b + 1) % 2 if isinstance(pair, int) and pair < 2 else b % 2

                def mask_scores(tp):
                    due = in_register(dve, 4 * j + tp + 1)
                    dve.wait_ge(scored, 1)
                    dve.wait_ge(scored, due)
                    for h in range(2):
                        for i in range(2):
                            c, t = column(tp, h, i), 2 * tp + i
                            dve.tensor_tensor_reduce(out=probs[:, h, t], in0=score[h][:, i * WIN:i * WIN + WIN],
                                                     in1=mask[:], scale=1.0, scalar=0.0, op0=ALU.mult, op1=ALU.max,
                                                     accum_out=row_max[:, c:c + 1]).then_inc(masked, 1)
                    dve.wait_ge(masked, 16 * j + 4 * tp + 4)
                    cols = slice(4 * tp, 4 * tp + 4)
                    dve.tensor_scalar(neg_max[:, cols], row_max[:, cols], -1.0, None, ALU.mult).then_inc(max_ready, 1)

                def denominators(half):
                    cols = slice(T * half, T * half + T)
                    dve.wait_ge(exp_done, 4 * j + 2 * half + 2)
                    dve.scalar_tensor_tensor(row_l[:, cols], e0[:, cols], float(N - WIN), row_sum[:, cols],
                                             ALU.mult, ALU.add).then_inc(l_ready, 1)
                    dve.wait_ge(l_ready, 2 * j + half + 1)
                    dve.reciprocal(inv_l[:, cols], row_l[:, cols]).then_inc(inv_ready, 1)
                    dve.wait_ge(inv_ready, 2 * j + half + 1)
                    dve.scalar_tensor_tensor(neg_e[:, cols], e0[:, cols], -1.0, inv_l[:, cols],
                                             ALU.mult, ALU.mult).then_inc(norm_ready, 1)

                def add_output(t):
                    dve.wait_ge(out_done, T * o + t + 1)
                    bank = fill[OUT_BANK[t] if proj else t % 2]
                    dve.tensor_tensor(acc[:, parity, t], bank[:], acc[:, parity, t], ALU.add).then_inc(out_added, 1)

                def hidden(q):
                    dve.wait_ge(ffn_relu, HQ * b + q + 1)
                    if q == 0:
                        dve.tensor_scalar(ffn_g, ffn_h[0], w2c[:, 0:1], b2c[:], ALU.mult, ALU.add).then_inc(ffn_acc, 1)
                    else:
                        dve.wait_ge(ffn_acc, HQ * b + q)
                        dve.scalar_tensor_tensor(ffn_g, ffn_h[q % 2], w2c[:, q:q + 1], ffn_g, ALU.mult, ALU.add) \
                            .then_inc(ffn_acc, 1)

                def qk_low(i):
                    part = [(qT[p][:] if i < 2 else kT[p][:, HALF:HALF + N])[:, i % 2 * LINE:i % 2 * LINE + LINE]
                            for p in (hi, lo)]
                    dve.wait_ge(qk_hi, 4 * n + i + 1)
                    dve.scalar_tensor_tensor(part[lo], fill[QK_BANK[i]][:], bias_qkv[:, Q_ + i // 2, pair],
                                             f32(part[hi]), ALU.add, ALU.subtract).then_inc(qk_lo, 1)

                def weights_low(u):
                    for k in range(2):
                        cols = slice(k * LINE, k * LINE + LINE)
                        dve.wait_ge(pT_hi, 8 * j + 2 * u + k + 1)
                        dve.tensor_tensor(pT[u % 2][lo][:, cols], pT_ps[k][:], f32(pT[u % 2][hi][:, cols]),
                                          ALU.subtract).then_inc(pT_lo, 1)

                def output_sum(u):
                    h, half = u % 2, u // 2
                    rows = slice(h * D, h * D + D)
                    dve.wait_ge(o_half, 4 * j + u + 1)
                    dve.wait_ge(v_back_ready, j + 1)
                    if h == 0 and begun(2 * j - 1 + half):
                        dve.wait_ge(oT_lo, 2 * j - 1 + half)
                    dve.scalar_tensor_tensor(o_sum[half][rows], o_ps[h][rows], v_back[rows], o_part[h][rows],
                                             ALU.add, ALU.add).then_inc(o_summed, 1)

                def values_low(i):
                    part = [v[:, 4 * i:4 * i + 4, :, p, :].rearrange("p c h d -> p (c h) d") for p in (hi, lo)]
                    dve.wait_ge(v_hi, 2 * n + i + 1)
                    dve.tensor_tensor(part[lo], fill[i][:].rearrange("p (c d) -> p c d", d=D), f32(part[hi]),
                                      ALU.subtract).then_inc(v_lo, 1)

                def x_low(b, items):
                    for i in items:
                        half, k = i // KC, i % KC
                        cols = slice(half * LINE, half * LINE + LINE)
                        dve.wait_ge(xT_hi, T * b + i + 1)
                        dve.tensor_tensor(xT[lo][:, k, cols], pT_ps[i % 2][:], f32(xT[hi][:, k, cols]), ALU.subtract) \
                            .then_inc(xT_lo, 1)

                if ln:
                    x_low(b, range(4 if attend else 0, 6))
                if attend:
                    mask_scores(0)
                if ffn_last:
                    hidden(3)
                if stats_next:
                    statistics(b + 1, range(0, 2))
                if out_proj:
                    add_output(0)
                if ln:
                    x_low(b, range(6, T))
                if attend:
                    mask_scores(1)
                if out_proj:
                    add_output(1)
                if ffn_last:
                    hidden(4)
                if stats_next:
                    statistics(b + 1, range(2, 5))
                if attend:
                    denominators(0)
                    mask_scores(2)
                if out_proj:
                    add_output(2)
                if stats_next:
                    statistics(b + 1, range(5, T))
                    mean_and_variance(b + 1)
                if ffn_last:
                    hidden(5)
                if proj:
                    qk_low(0)
                if out_proj:
                    add_output(3)
                if attend:
                    mask_scores(3)
                if attend:
                    weights_low(0)
                if out_proj and not ffn_first:
                    add_output(4)
                for half in range(2) if ffn_first else ():
                    line = slice(half * LINE, half * LINE + LINE)
                    dve.wait_ge(ffn_half, 2 * b + half + 1)
                    dve.scalar_tensor_tensor(ffn_s[:, line], fill[1 - half][:], ffn_bin[:], ffn_part[:, line],
                                             ALU.add, ALU.add).then_inc(ffn_s_in, 1)
                if attend:
                    denominators(1)
                if out_proj and ffn_first:
                    add_output(4)
                if proj and not ffn_first:
                    qk_low(1)
                if attend:
                    weights_low(1)
                    output_sum(0)
                if proj and ffn_first:
                    qk_low(1)
                if ffn_first or ffn_last:
                    hidden(0 if ffn_first else 6)
                if proj:
                    dve.wait_ge(v_in, 2 * n + 2)
                    dve.tensor_tensor(v_mean[:, 0:1], v_sums[:, 0:1], v_sums[:, 1:2], ALU.add).then_inc(v_stat, 1)
                    dve.wait_ge(v_stat, 3 * n + 1)
                    dve.tensor_tensor(v_mean[:, 1:2], v_mean[:, 0:1], v_sums[:, 2:3], ALU.add).then_inc(v_stat, 1)
                    dve.wait_ge(v_stat, 3 * n + 2)
                    dve.tensor_scalar(v_new[:], v_mean[:, 1:2], 1.0 / N, None, ALU.mult).then_inc(v_stat, 1)
                    dve.wait_ge(v_stat, 3 * n + 3)
                    dve.tensor_scalar(vT[:], vT[:], v_new[:], None, ALU.subtract).then_inc(v_centered, 1)
                if out_proj:
                    add_output(5)
                if proj:
                    qk_low(2)
                if attend:
                    weights_low(2)
                    output_sum(1)
                if out_proj:
                    add_output(6)
                if ffn_first or ffn_last:
                    hidden(1 if ffn_first else 7)
                if attend:
                    weights_low(3)
                if ffn_first:
                    hidden(2)
                if ffn_last:
                    dve.wait_ge(ffn_g_hi, b + 1)
                    dve.tensor_tensor(ffn_g_parts[lo][:], ffn_g, f32(ffn_g_parts[hi][:]), ALU.subtract) \
                        .then_inc(ffn_g_lo, 1)
                if out_proj and not ln_next:
                    add_output(7)
                if proj:
                    qk_low(3)
                if ln_next:
                    x_low(b + 1, range(0, 2))
                    add_output(7)
                if attend:
                    output_sum(2)
                if ln_next:
                    x_low(b + 1, range(2, 4))
                if proj:
                    values_low(0)
                if attend:
                    output_sum(3)
                if proj:
                    values_low(1)
                if proj:
                    if attend:
                        dve.wait_ge(o_summed, 4 * j + 4)
                    dve.tensor_tensor(v_back[:], v_new[:], bias_qkv[:, V_, pair], ALU.add).then_inc(v_back_ready, 1)
                for t in range(T) if ffn_last else ():
                    dve.wait_ge(ffn_out, T * b + t + 1)
                    dve.wait_ge(bias_added, T * b + t + 1)
                    dve.tensor_tensor(acc[:, b % 2, t], ffn_banks[t % 4][:], acc[:, b % 2, t], ALU.add) \
                        .then_inc(ffn_added, 1)

            run_steps(dve, step)

        @block.tensor
        def _(pe):
            pe.wait_ge(pool_set, 6)
            pe.wait_ge(dve_set, 5)
            pe.wait_ge(win_ready, 2)
            pe.wait_ge(const_in, 16 * N_CONST)
            pe.transpose(score[0][:, 0:3 * PAIRS], bias_rows[:], ident[0:3 * PAIRS, 0:3 * PAIRS]).then_inc(bias_T, 1)

            def step(n, b, pair, proj=True, attend=True, out_proj=True, ln=False, ln_next=False,
                     ffn_first=False, ffn_last=False, after_ffn=False, **_):
                j, o = n - 1, n - 2
                def scores(tp):
                    if tp == 0:
                        pe.wait_ge(qk_lo, 4 * j + 4)
                    if begun(16 * j + 4 * tp):
                        pe.wait_ge(masked, 16 * j + 4 * tp)
                    for i in range(2):
                        t = 2 * tp + i
                        for a, (qp, kp) in enumerate(PASSES):
                            for h in range(2):
                                rows = slice(h * D, h * D + D)
                                last = pe.matmul(score[h][:, i * WIN:i * WIN + WIN], qT[qp][rows, t * P:t * P + P],
                                                 kT[kp][rows, t * P:t * P + WIN], start=(a == 0), stop=(a == 2))
                    last.then_inc(scored, 1)

                def project(i, half, done, dst):
                    pe.wait_ge(w_lo, 3 * n + i + 1)
                    for k in range(KC):
                        for a, (wp, xp) in enumerate(PASSES):
                            last = pe.matmul(dst[:], w[wp][:, i, k], xT[xp][:, k, half * LINE:half * LINE + LINE],
                                             start=(k == 0 and a == 0), stop=(k == KC - 1 and a == 2))
                    last.then_inc(done, 1)

                def project_out(t):
                    if t == 0:
                        pe.wait_ge(wo_lo, o + 1)
                    if t % 4 == 0:
                        pe.wait_ge(oT_lo, 2 * o + t // 4 + 1)
                    dst = fill[OUT_BANK[t] if proj else t % 2]
                    for a, (op, wp) in enumerate(PASSES):
                        last = pe.matmul(dst[:], oT[op][:, t * P:t * P + P], wo[wp][:], start=(a == 0), stop=(a == 2))
                    last.then_inc(out_done, 1)

                def project_out_last(t):
                    if t >= 2:
                        pe.wait_ge(out_added, T * o + t - 1)
                    elif attend:
                        pe.wait_ge(v_lo, 2 * n - 1 + t)
                    else:
                        pe.wait_ge(out_added, T * o)
                    project_out(t)

                def transpose_x(b, i):
                    half, k = i // KC, i % KC
                    pe.wait_ge(xn_ready, T * b + 4 * half + 4)
                    if i >= 2:
                        pe.wait_ge(xT_lo, T * b + i - 1)
                    for t in tiles_of(half):
                        last = pe.transpose(pT_ps[i % 2][:, t % 4 * P:t % 4 * P + P], xn[:, t, k * P:k * P + P],
                                            ident[:])
                    last.then_inc(xT_done, 1)

                def network_in(half):
                    for k in range(KC):
                        for xp in (hi, lo):
                            last = pe.matmul(fill[1 - half][:], win[:, k].rearrange("p u m -> p (u m)"),
                                             xT[xp][:, k, half * LINE:half * LINE + LINE],
                                             start=(k == 0 and xp == hi), stop=(k == KC - 1 and xp == lo))
                    last.then_inc(ffn_in, 1)

                def transpose_values(i):
                    for c in range(4):
                        last = pe.transpose(fill[i][:, c * P:c * P + P], vT[:, (4 * i + c) * P:(4 * i + c + 1) * P],
                                            ident[:])
                    last.then_inc(v_T, 1)

                def transpose_weights(u):
                    half, h = u // 2, u % 2
                    pe.wait_ge(normed, 16 * j + 4 * u + 4)
                    for i in range(8):
                        t, c, k = 4 * half + i // 2, i % 2, i // 4
                        if i % 4 == 0 and begun(8 * j + 2 * u + k - 1):
                            pe.wait_ge(pT_lo, 8 * j + 2 * u + k - 1)
                        last = pe.transpose(pT_ps[k][:, i % 4 * P:i % 4 * P + P], probs[:, h, t, c * P:c * P + P],
                                            ident[:])
                        if i % 4 == 3:
                            last.then_inc(p_T, 1)

                def weigh_values(u):
                    half, h = u // 2, u % 2
                    pe.wait_ge(pT_lo, 8 * j + 2 * u + 2)
                    if u == 0:
                        pe.wait_ge(v_lo, 2 * j + 2)
                    if begun(4 * j + u - 1):
                        pe.wait_ge(o_summed, 4 * j + u - 1)
                    for k in range(5):
                        first, end = max(2 * k - 1, 0), min(2 * k + 1, 8)
                        q0 = max(k - 1, 0) * P
                        for part in (hi, lo):
                            last = pe.matmul(o_ps[h][:, q0:q0 + (end - first) * P],
                                             v[:, (4 * half + k) % T, h].rearrange("p a d -> p (a d)"),
                                             pT[h][part][:, first * P:end * P], start=(k == 0 and part == hi),
                                             stop=(k == 4 and part == lo), skip_group_check=True)
                    last.then_inc(pv_done, 1)

                if ln and not attend:
                    for i in range(0, 4):
                        transpose_x(b, i)
                if attend:
                    scores(0)
                if ln:
                    transpose_x(b, 4)
                    transpose_x(b, 5)
                if proj:
                    if ln:
                        pe.wait_ge(xT_lo, T * b + KC)
                    if begun(2 * n - 1):
                        pe.wait_ge(v_lo, 2 * n - 1)
                    if after_ffn:
                        pe.wait_ge(ffn_added, T * b + T - 1)
                    project(V_, 0, v_proj, fill[0])
                if out_proj and not proj:
                    project_out_last(0)
                elif out_proj:
                    pe.wait_ge(v_lo, 2 * n)
                    if after_ffn:
                        pe.wait_ge(ffn_added, T * b + T)
                    project_out(0)
                if ln:
                    transpose_x(b, 6)
                    transpose_x(b, 7)
                if attend:
                    scores(1)
                if out_proj and not proj:
                    project_out_last(1)
                elif out_proj:
                    pe.wait_ge(v_in, 2 * n + 1)
                    project_out(1)
                if proj:
                    if ln:
                        pe.wait_ge(xT_lo, T * b + T)
                    if out_proj:
                        pe.wait_ge(out_added, T * o + 1)
                    elif begun(2 * n):
                        pe.wait_ge(v_lo, 2 * n)
                    project(V_, 1, v_proj, fill[1])
                if attend:
                    scores(2)
                if out_proj and not proj:
                    project_out_last(2)
                elif out_proj:
                    pe.wait_ge(out_added, T * o + 2)
                    project_out(2)
                if proj:
                    pe.wait_ge(v_in, 2 * n + 2)
                    project(Q_, 0, qk_proj, fill[QK_BANK[0]])
                if attend:
                    scores(3)
                if out_proj and not proj:
                    project_out_last(3)
                elif out_proj:
                    pe.wait_ge(out_added, T * o + 3)
                    project_out(3)
                if attend:
                    transpose_weights(0)
                if ffn_first:
                    pe.wait_ge(qk_lo, 4 * n + 1)
                    network_in(0)
                    if out_proj:
                        pe.wait_ge(out_added, T * o + 4)
                    network_in(1)
                if attend and ffn_first:
                    transpose_weights(1)
                    weigh_values(0)
                if out_proj and not proj:
                    project_out_last(4)
                elif out_proj:
                    if ffn_first:
                        pe.wait_ge(ffn_s_in, 2 * b + 1)
                    else:
                        pe.wait_ge(qk_lo, 4 * n + 1)
                    project_out(4)
                if proj:
                    if ffn_first:
                        pe.wait_ge(ffn_s_in, 2 * b + 2)
                    elif out_proj:
                        pe.wait_ge(out_added, T * o + 4)
                    else:
                        pe.wait_ge(v_in, 2 * n + 1)
                    project(Q_, 1, qk_proj, fill[QK_BANK[1]])
                if attend and not ffn_first:
                    transpose_weights(1)
                    weigh_values(0)
                if proj:
                    if out_proj:
                        pe.wait_ge(out_added, T * o + 5)
                    else:
                        pe.wait_ge(qk_lo, 4 * n + 1)
                    project(K_, 0, qk_proj, fill[QK_BANK[2]])
                if out_proj and not proj:
                    project_out_last(5)
                elif out_proj:
                    pe.wait_ge(qk_lo, 4 * n + 2)
                    project_out(5)
                if attend:
                    transpose_weights(2)
                    weigh_values(1)
                if out_proj and not proj:
                    project_out_last(6)
                elif out_proj:
                    pe.wait_ge(out_added, T * o + 6)
                    project_out(6)
                if attend:
                    transpose_weights(3)
                if proj:
                    pe.wait_ge(qk_lo, 4 * n + 3)
                    project(K_, 1, qk_proj, fill[QK_BANK[3]])
                if ln_next:
                    pe.wait_ge(pT_lo, 8 * j + 8)
                    transpose_x(b + 1, 0)
                    transpose_x(b + 1, 1)
                if out_proj and not proj:
                    project_out_last(7)
                elif out_proj:
                    pe.wait_ge(out_added, T * o + 7)
                    project_out(7)
                if attend:
                    weigh_values(2)
                if ln_next:
                    transpose_x(b + 1, 2)
                    transpose_x(b + 1, 3)
                if attend:
                    weigh_values(3)
                if proj:
                    pe.wait_ge(v_centered, n + 1)
                    if out_proj:
                        pe.wait_ge(out_added, T * o + T)
                    transpose_values(0)
                    pe.wait_ge(qk_lo, 4 * n + 4)
                    transpose_values(1)
                for t in range(T) if ffn_last else ():
                    if t == 0:
                        pe.wait_ge(ffn_g_lo, b + 1)
                    elif t in (2, 3):
                        pe.wait_ge(v_lo, 2 * n - 1 + t)
                    elif t >= 4:
                        pe.wait_ge(ffn_added, T * b + t - 3)
                    for a, (gp, wp) in enumerate(PASSES):
                        last = pe.matmul(ffn_banks[t % 4][:], ffn_g_parts[gp][:, t * P:t * P + P], wout[wp][:],
                                         start=(a == 0), stop=(a == 2))
                    last.then_inc(ffn_out, 1)

            run_steps(pe, step)


_INS = ["L0_attn_x", "L0_attn_Wq", "L0_attn_bq", "L0_attn_Wk", "L0_attn_bk", "L0_attn_Wv", "L0_attn_bv", "L0_attn_Wo",
        "L0_attn_bo", "L0_ffn_Win", "L0_ffn_bin_", "L0_ffn_W1", "L0_ffn_b1", "L0_ffn_W2", "L0_ffn_b2", "L0_ffn_Wout",
        "L0_ffn_bout"]


def kernel(**inputs):
    import numpy as np
    import concourse.bacc as bacc
    from concourse.bass_utils import run_bass_kernel_spmd

    nc = bacc.Bacc("TRN2", target_bir_lowering=False, num_devices=1)
    arrays, args = {}, []
    for name in _INS:
        a = np.ascontiguousarray(inputs[name])
        arrays[f"in_{name}"] = a
        args.append(nc.dram_tensor(f"in_{name}", a.shape, mybir.dt.from_np(a.dtype), kind="ExternalInput").ap())
    shape = inputs["L0_attn_x"].shape
    args.append(nc.dram_tensor("out_x", shape, F32, kind="ExternalOutput").ap())
    band_attention_ffn(nc, *args)
    return run_bass_kernel_spmd(nc, [arrays], core_ids=[0]).results[0]["out_x"]
```
